# Optimizing a Trainium2 kernel written in Bass

```python
import numpy as np
import jax
import jax.numpy as jnp

def _softmax(x, axis=-1):
    return jax.nn.softmax(x, axis=axis)

def _gelu(x):
    return jax.nn.gelu(x, approximate=True)

def _silu(x):
    return jax.nn.silu(x)

def _sigmoid(x):
    return jax.nn.sigmoid(x)

def _layernorm(x, axis=-1, eps=1e-05):
    m = jnp.mean(x, axis=axis, keepdims=True)
    v = jnp.var(x, axis=axis, keepdims=True)
    return (x - m) / jnp.sqrt(v + eps)

def _scatter_add(tgt, idx, src, axis=0):
    return tgt.at[idx].add(src)

def _segment_sum(src, seg, n):
    return jax.ops.segment_sum(src, seg, n)
kernel_name = 'mk_seq_postln_d1_jaxref_r2_901146'

def setup_inputs(seed: int=0):
    np.random.seed(seed)
    _w = jnp.asarray

    def _L0_attn_setup():
        import jax, jax.numpy as jnp
        import numpy as np
        BATCH, SEQ, D_MODEL, D_STATE = (8, 2048, 512, 16)
        LN_EPS = 1e-05
        key = jax.random.key(seed)
        ks = jax.random.split(key, 8)
        lin = lambda k, i, o: jax.random.normal(k, (i, o), jnp.float32) * (1.0 / np.sqrt(i))
        return {'x': jax.random.normal(ks[0], (BATCH, SEQ, D_MODEL), jnp.float32), 'ln_gamma': jnp.ones((D_MODEL,), jnp.float32), 'ln_beta': jnp.zeros((D_MODEL,), jnp.float32), 'A': jax.random.normal(ks[1], (D_STATE, D_STATE), jnp.float32) * 0.01, 'C': jax.random.normal(ks[2], (D_STATE, D_MODEL), jnp.float32) * 0.01, 'w_delta': lin(ks[3], D_MODEL, D_STATE), 'b_delta': jnp.zeros((D_STATE,), jnp.float32), 'w_in': lin(ks[4], D_MODEL, D_STATE), 'b_in': jnp.zeros((D_STATE,), jnp.float32), 'w_gate': lin(ks[5], D_MODEL, D_MODEL), 'b_gate': jnp.zeros((D_MODEL,), jnp.float32)}
    _L0_attn_in = _L0_attn_setup()

    def _L0_ffn_setup():
        import jax, jax.numpy as jnp
        import numpy as np
        B, N, D = (4, 1024, 512)
        SPARSITY = 0.01
        key = jax.random.key(seed)
        k1, k2, k3 = jax.random.split(key, 3)
        x = jax.random.normal(k1, (B, N, D), dtype=jnp.float32)
        spatial = jax.random.normal(k2, (D, D), dtype=jnp.float32) * 0.02
        freq = jnp.fft.fft(spatial, axis=-1)
        k = int(D * SPARSITY)
        mag = jnp.abs(freq)
        kth = jax.lax.top_k(mag, k)[0][:, -1:]
        w_sparse = jnp.where(mag >= kth, freq, 0.0 + 0j)
        bias = jax.random.normal(k3, (D,), dtype=jnp.float32) * 0.01
        return {'x': x, 'w_freq_real': jnp.real(w_sparse).astype(jnp.float32), 'w_freq_imag': jnp.imag(w_sparse).astype(jnp.float32), 'bias': bias}
    _L0_ffn_in = _L0_ffn_setup()
    _d = {'L0_attn_x': _L0_attn_in['x'], 'L0_attn_ln_gamma': _L0_attn_in['ln_gamma'], 'L0_attn_ln_beta': _L0_attn_in['ln_beta'], 'L0_attn_A': _L0_attn_in['A'], 'L0_attn_C': _L0_attn_in['C'], 'L0_attn_w_delta': _L0_attn_in['w_delta'], 'L0_attn_b_delta': _L0_attn_in['b_delta'], 'L0_attn_w_in': _L0_attn_in['w_in'], 'L0_attn_b_in': _L0_attn_in['b_in'], 'L0_attn_w_gate': _L0_attn_in['w_gate'], 'L0_attn_b_gate': _L0_attn_in['b_gate'], 'L0_ffn_w_freq_real': _L0_ffn_in['w_freq_real'], 'L0_ffn_w_freq_imag': _L0_ffn_in['w_freq_imag'], 'L0_ffn_bias': _L0_ffn_in['bias']}
    _x0 = _d['L0_attn_x']
    _d['L0_attn_x'] = jax.random.normal(jax.random.fold_in(jax.random.key(seed), 1), (8, 2048, 512), dtype=_x0.dtype)
    del _x0
    return _d

def reference(L0_attn_x, L0_attn_ln_gamma, L0_attn_ln_beta, L0_attn_A, L0_attn_C, L0_attn_w_delta, L0_attn_b_delta, L0_attn_w_in, L0_attn_b_in, L0_attn_w_gate, L0_attn_b_gate, L0_ffn_w_freq_real, L0_ffn_w_freq_imag, L0_ffn_bias):

    def _L0_attn_ref(x, ln_gamma, ln_beta, A, C, w_delta, b_delta, w_in, b_in, w_gate, b_gate):
        import jax, jax.numpy as jnp
        import numpy as np
        BATCH, SEQ, D_MODEL, D_STATE = (8, 2048, 512, 16)
        LN_EPS = 1e-05
        mu = jnp.mean(x, axis=-1, keepdims=True)
        var = jnp.var(x, axis=-1, keepdims=True)
        xn = (x - mu) / jnp.sqrt(var + LN_EPS) * ln_gamma + ln_beta
        delta = jax.nn.sigmoid(jnp.einsum('btd,ds->bts', xn, w_delta) + b_delta)
        B_t = jnp.einsum('btd,ds->bts', xn, w_in) + b_in
        gate = jax.nn.sigmoid(jnp.einsum('btd,de->bte', xn, w_gate) + b_gate)

        def step(h, inp):
            d_t, b_t = inp
            h_new = jnp.tanh(h * d_t @ A + b_t)
            return (h_new, h_new)
        h0 = jnp.zeros((x.shape[0], A.shape[0]), x.dtype)
        _, hs = jax.lax.scan(step, h0, (jnp.swapaxes(delta, 0, 1), jnp.swapaxes(B_t, 0, 1)))
        y = jnp.swapaxes(jnp.einsum('tbs,se->tbe', hs, C), 0, 1) * gate
        return y + x

    def _L0_ffn_ref(x, w_freq_real, w_freq_imag, bias):
        import jax, jax.numpy as jnp
        import numpy as np
        B, N, D = (4, 1024, 512)
        SPARSITY = 0.01
        w = jax.lax.complex(w_freq_real, w_freq_imag)
        x_freq = jnp.fft.fft(x, axis=-1)
        y_freq = jnp.einsum('bnd,do->bno', x_freq, w)
        y = jnp.real(jnp.fft.ifft(y_freq, axis=-1))
        return y + bias
    x = L0_attn_x
    x = _layernorm(x + _L0_attn_ref(x, L0_attn_ln_gamma, L0_attn_ln_beta, L0_attn_A, L0_attn_C, L0_attn_w_delta, L0_attn_b_delta, L0_attn_w_in, L0_attn_b_in, L0_attn_w_gate, L0_attn_b_gate), axis=-1)
    x = _layernorm(x + _L0_ffn_ref(x, L0_ffn_w_freq_real, L0_ffn_w_freq_imag, L0_ffn_bias), axis=-1)
    return x

_drawn_inputs = setup_inputs


def setup_inputs(seed=0):
    import zlib

    import numpy as np

    out = dict(_drawn_inputs(seed))
    spreads = {'L0_attn_ln_gamma': (1.0, 0.6),
     'L0_attn_ln_beta': (0.0, 0.8),
     'L0_attn_b_delta': (0.0, 2.0),
     'L0_attn_b_in': (0.0, 2.0),
     'L0_attn_b_gate': (0.0, 2.0)}
    factors = {'L0_attn_A': 64.0,
     'L0_attn_C': 7.912,
     'L0_attn_w_delta': 64.0,
     'L0_attn_w_in': 7.979,
     'L0_attn_w_gate': 8.0,
     'L0_ffn_bias': 8.0}
    for name, (base, spread) in spreads.items():
        noise = np.random.default_rng([zlib.crc32(name.encode()), seed]).standard_normal(out[name].shape)
        drawn = base * np.exp(spread * noise) if base else spread * noise
        out[name] = jnp.asarray(drawn.astype(out[name].dtype))
    for name, factor in factors.items():
        out[name] = (out[name] * factor).astype(out[name].dtype)
    return out
```

```python
from contextlib import ExitStack

import numpy as np

import concourse.bass as bass
from concourse import mybir

P = 128
BATCH, SEQ, D = 8, 2048, 512
STATE = 16
KT = D // P
GROUPS = 4
GROUP_ROWS = BATCH * SEQ // GROUPS
QUADS = GROUP_ROWS // P
TILES = QUADS * GROUPS
OCTETS = TILES // 8
HALF = D // 2 + 1
CHUNK = 16
LANES = GROUP_ROWS // CHUNK
BATCH_LANES = SEQ // CHUNK
LN_EPS = 1e-5
SPLIT_TOP = 2.0 ** 14
ROW_SCALE = 2.0 ** 11
STATE_SCALE = 2.0 ** 14

ALU = mybir.AluOpType
ACT = mybir.ActivationFunctionType
F32 = mybir.dt.float32
F16 = mybir.dt.float16
I32 = mybir.dt.int32
AX = mybir.AxisListType
ABSMAX = bass.bass_isa.ReduceOp.absmax

C_IDENT, C_SELECT, C_MASK, C_LOROW, C_WIDTH = 0, P, 2 * P, 2 * P + GROUPS, 2 * P + GROUPS + 1


def exists(n):
    return not isinstance(n, int) or 0 <= n < TILES


def before(n, k):
    return not isinstance(n, int) or n >= k


def run_slots(engine, first, last, slot):
    for n in range(first, 8):
        slot(n, n % 8, n // 8)
    with engine.Fori(1, OCTETS - 1) as v:
        for k in range(8):
            slot(v * 8 + k, k, v)
    for n in range(TILES - 8, last + 1):
        slot(n, n % 8, n // 8)


def build(nc, x, gamma, beta, A, C, w_delta, b_delta, w_in, b_in, w_gate, b_gate, w_re, w_im,
          ffn_bias, consts, dft, out, gate_dram):
    ctx = ExitStack()
    with ctx:
        def sb(name, shape, dt=F32):
            return ctx.enter_context(nc.sbuf_tensor(name, shape, dt))

        def sem(name):
            return ctx.enter_context(nc.semaphore(name))

        x_sb = sb("x_sb", [P, 2, GROUPS, D])
        gate_sb = sb("gate_sb", [P, 2, GROUPS, D])
        out_sb = sb("out_sb", [P, 2, GROUPS, D])
        norm_sb = sb("norm_sb", [P, 4, D])
        hi_sb = sb("hi_sb", [P, 2, KT, P], F16)
        lo_sb = sb("lo_sb", [P, 2, KT, P], F16)
        gsum_sb = sb("gsum_sb", [P, 2, D])
        wg_raw = sb("wg_raw", [P, KT, D])
        wg_fold = sb("wg_fold", [P, KT, D])
        m_sb, w_sb, zb_sb = wg_fold, wg_fold, wg_raw
        wg_hi = sb("wg_hi", [P, KT, D], F16)
        wg_lo = sb("wg_lo", [P, KT, D], F16)
        wp_raw = sb("wp_raw", [P, KT, 2, STATE])
        wp_rep = sb("wp_rep", [P, KT, GROUPS, 2 * STATE])
        wp_fold = sb("wp_fold", [P, KT, 2 * STATE])
        wp_hi = sb("wp_hi", [P, KT, 2 * STATE], F16)
        wp_lo = sb("wp_lo", [P, KT, 2 * STATE], F16)
        gamma_sb = sb("gamma_sb", [P, KT])
        beta_sb = sb("beta_sb", [P, KT])
        beta_rep = sb("beta_rep", [P, KT, P])
        bias_row = sb("bias_row", [1, 2, D])
        ones_sb = sb("ones_sb", [P, P])
        gbias_sb = sb("gbias_sb", [P, D])
        fbias_sb = sb("fbias_sb", [P, D])
        zb_in = sb("zb_in", [P, 1])
        zbias = sb("zbias", [P, 1])
        cst = sb("cst", [P, C_WIDTH])
        ident = cst[:, C_IDENT:C_IDENT + P]
        select = cst[:, C_SELECT:C_SELECT + P]
        scan_a = sb("scan_a", [P, P])
        c_rep = sb("c_rep", [P, D])
        c_hi = sb("c_hi", [P, D], F16)
        c_lo = sb("c_lo", [P, D], F16)
        cg_hi = sb("cg_hi", [P, GROUPS, D], F16)
        cg_lo = sb("cg_lo", [P, GROUPS, D], F16)
        amax = sb("amax", [P, 4])
        amax_all = sb("amax_all", [P, 4])
        amax_pos = sb("amax_pos", [P, 4])
        pow2 = sb("pow2", [P, 4])
        pow2_inv = sb("pow2_inv", [P, 4])
        scale = sb("scale", [P, 4])
        unscale = sb("unscale", [P, 4])
        zrow = sb("zrow", [P, P])
        z_sb = sb("z_sb", [P, GROUP_ROWS])
        del_sb = sb("del_sb", [P, GROUP_ROWS])
        h_sb = sb("h_sb", [P, GROUP_ROWS])
        h16 = sb("h16", [P, GROUP_ROWS], F16)
        hd = sb("hd", [P, LANES])
        hd_first = sb("hd_first", [P, LANES])
        ends = sb("ends", [P, LANES])
        differ = sb("differ", [P, LANES])
        n_differ = sb("n_differ", [P, 1])
        flag = sb("flag", [1, 1], I32)
        w_re_sb = sb("w_re_sb", [P, KT, D])
        w_im_sb = sb("w_im_sb", [P, KT, D])
        cos_sb = sb("cos_sb", [P, KT, HALF])
        sin_sb = sb("sin_sb", [P, KT, HALF])
        even_sb = sb("even_sb", [P, 2, 2, HALF])
        pt_sb = out_sb[:, 0]
        qt_sb = out_sb[:, 1]
        m_split = w_re_sb[:].bitcast(F16)
        m_hi, m_lo = m_split[:, :, 0:D], m_split[:, :, D:2 * D]
        bn = sb("bn", [P, 4, 6])
        mv = sb("mv", [P, 4, 2])
        veps = sb("veps", [P, 4])
        rstd = sb("rstd", [P, 4])
        c_eps = sb("c_eps", [P, 1])
        c_eps4 = sb("c_eps4", [P, 1])
        c_half = sb("c_half", [P, 1])
        wsum = sb("wsum", [P, 4])
        negmu = sb("negmu", [P, 4])
        vsum = sb("vsum", [P, 4])
        var2 = sb("var2", [P, 4])
        rnorm2 = sb("rnorm2", [P, 4])
        rstd2 = sb("rstd2", [P, 4])
        c_mean = sb("c_mean", [P, 1])
        c_epsd = sb("c_epsd", [P, 1])
        c_rootd = sb("c_rootd", [P, 1])
        nbias2 = sb("nbias2", [P, 4])

        bank = [ctx.enter_context(nc.psum_tensor(f"bank{i}", [P, 512], F32)) for i in range(8)]
        ps_t, ps_g, ps_z, ps_x, ps_y = bank[0:2], bank[2:4], bank[4:6], bank[6], bank[4:6]

        def tiles_of(t):
            return t.rearrange("(g u p) d -> u p g d", g=GROUPS, p=P)

        x_v, out_v, gate_v = tiles_of(x), tiles_of(out), tiles_of(gate_dram)

        s_wa = sem("weights_loaded")
        s_wb = sem("fourier_loaded")
        s_pool_const = sem("pool_constants")
        s_dve = sem("dve_step")
        s_amax = sem("amax_ready")
        s_amax_all = sem("amax_reduced")
        s_brep = sem("beta_replicated")
        s_bias_mm = sem("bias_products")
        s_wready = sem("weights_split")
        s_xl = [sem(f"x_loaded{i}") for i in range(2)]
        s_gst = [sem(f"gate_stored{i}") for i in range(2)]
        s_bn = sem("a_bn")
        s_aggr = sem("a_variance")
        s_veps = sem("a_variance_eps")
        s_rstd = sem("a_rstd")
        s_norm = sem("a_norm")
        s_t = sem("a_transposed")
        s_hi = sem("a_hi")
        s_lo = sem("a_lo")
        s_gate = sem("a_gate_products")
        s_proj = sem("a_projections")
        s_gsum = sem("a_gate_logits")
        s_gsig = sem("a_gate")
        s_zrow = sem("a_zrow")
        s_zt = sem("a_z_transposed")
        s_del = sem("a_delta")
        s_z = sem("a_z")
        s_e_mm = sem("m_products")
        s_even = sem("m_even_copied")
        s_pq = sem("m_pq")
        s_u_mm = sem("m_products2")
        s_u = sem("m_u_copied")
        s_m = sem("m_ready")
        s_msplit = sem("m_split")
        s_hd = sem("scan_hd")
        s_pre = sem("scan_pre")
        s_h = sem("scan_h")
        s_cmp = sem("scan_compared")
        s_cnt = sem("scan_counted")
        s_flag = sem("scan_flag")
        s_dscan = sem("scan_dve")
        s_h16 = sem("h16_ready")
        s_bx = [sem(f"b_x_loaded{i}") for i in range(2)]
        s_bg = [sem(f"b_gate_loaded{i}") for i in range(2)]
        s_bst = [sem(f"b_stored{i}") for i in range(2)]
        s_y = sem("b_y")
        s_gy = sem("b_gated")
        s_v = sem("b_v")
        s_bbn = sem("b_bn")
        s_baggr = sem("b_variance")
        s_bveps = sem("b_variance_eps")
        s_brstd = sem("b_rstd")
        s_bnorm = sem("b_norm")
        s_bt = sem("b_transposed")
        s_bhi = sem("b_hi")
        s_blo = sem("b_lo")
        s_f = sem("b_ffn_products")
        s_zb = sem("b_residual")
        s_w = sem("b_w")
        s_negmu = sem("b_negmu")
        s_sq = sem("b_squares")
        s_var2 = sem("b_var2")
        s_rnorm2 = sem("b_rnorm2")
        s_rstd2 = sem("b_rstd2")
        s_nb2 = sem("b_nbias2")
        s_out = sem("b_out")

        block = ctx.enter_context(nc.Block())
        N_WA = [0]

        @block.sync
        def _(sp):
            def load_x(u, par, loaded):
                sp.dma_start(x_sb[:, par], x_v[u]).then_inc(loaded[par], 16)

            def first_pass(u, par, v):
                if not isinstance(u, int) or u + 2 < QUADS:
                    sp.wait_ge(s_norm, (u + 1) * 4)
                    load_x(u + 2, par, s_xl)
                sp.wait_ge(s_gsig, (u + 1) * 4)
                sp.dma_start(gate_v[u], gate_sb[:, par]).then_inc(s_gst[par], 16)

            load_x(0, 0, s_xl)
            load_x(1, 1, s_xl)
            with sp.Fori(0, OCTETS - 1) as v:
                first_pass(v * 2, 0, v)
                first_pass(v * 2 + 1, 1, v)
            first_pass(QUADS - 2, 0, OCTETS - 1)
            first_pass(QUADS - 1, 1, OCTETS - 1)

            def load_b(u, par):
                load_x(u, par, s_bx)
                sp.dma_start(gate_sb[:, par], gate_v[u]).then_inc(s_bg[par], 16)

            def second_pass(u, par):
                if not isinstance(u, int) or u + 2 < QUADS:
                    sp.wait_ge(s_bnorm, (u + 1) * 4)
                    load_b(u + 2, par)
                sp.wait_ge(s_out, (u + 1) * 4)
                sp.dma_start(out_v[u], out_sb[:, par]).then_inc(s_bst[par], 16)

            sp.wait_ge(s_norm, TILES)
            sp.wait_ge(s_gst[0], 16 * OCTETS)
            sp.wait_ge(s_gst[1], 16 * OCTETS)
            load_b(0, 0)
            load_b(1, 1)
            with sp.Fori(0, OCTETS - 1) as v:
                second_pass(v * 2, 0)
                second_pass(v * 2 + 1, 1)
            second_pass(QUADS - 2, 0)
            second_pass(QUADS - 1, 1)
            sp.wait_ge(s_bst[0], 16 * OCTETS)
            sp.wait_ge(s_bst[1], 16 * OCTETS)

        WA_LOADS = [
            (wg_raw[:], w_gate.rearrange("(t p) n -> p t n", p=P)),
            (wp_raw[:, :, 0, :], w_delta.rearrange("(t p) n -> p t n", p=P)),
            (wp_raw[:, :, 1, :], w_in.rearrange("(t p) n -> p t n", p=P)),
            (gamma_sb[:], gamma),
            (beta_sb[:], beta),
            (bias_row[0:1, 0, :], b_gate.rearrange("(a n) -> a n", a=1)),
            (bias_row[0:1, 1, :], ffn_bias.rearrange("(a n) -> a n", a=1)),
            (cst[:], consts),
        ]
        for g in range(GROUPS):
            p0, p1 = g * 2 * STATE, g * 2 * STATE + STATE
            WA_LOADS += [
                (zb_in[p0:p0 + STATE, :], b_delta.rearrange("(n a) -> n a", a=1)),
                (zb_in[p1:p1 + STATE, :], b_in.rearrange("(n a) -> n a", a=1)),
                (c_rep[p0:p0 + STATE, :], C),
                (c_rep[p1:p1 + STATE, :], C),
            ]
        SCAN_A_LOADS = [(scan_a[g * 32:g * 32 + STATE, g * 32 + r * STATE:g * 32 + (r + 1) * STATE], A)
                        for g in range(GROUPS) for r in range(2)]
        WB_LOADS = [
            (w_re_sb[:], w_re.rearrange("(t p) n -> p t n", p=P)),
            (w_im_sb[:], w_im.rearrange("(t p) n -> p t n", p=P)),
            (cos_sb[:], dft[0].rearrange("(t p) n -> p t n", p=P)),
            (sin_sb[:], dft[1].rearrange("(t p) n -> p t n", p=P)),
        ]

        @block.scalar
        def _(act):
            for dst, src in WA_LOADS:
                act.dma_start(dst, src).then_inc(s_wa, 16)
            act.wait_ge(s_pool_const, 1)
            for dst, src in SCAN_A_LOADS + WB_LOADS:
                act.dma_start(dst, src).then_inc(s_wb, 16)

            def hi(n, k):
                act.wait_ge(s_t, n + 1)
                if before(n, 2):
                    act.wait_ge(s_proj, n - 1)
                nc.scalar.activation(hi_sb[:, k % 2], ps_t[k % 2][:], ACT.Copy,
                                     scale=ROW_SCALE).then_inc(s_hi, 1)

            def sigmoid_gate(n, k, v):
                act.wait_ge(s_gsum, n + 1)
                if k % 4 == 0 and before(n, 8):
                    act.wait_ge(s_gst[k // 4], v * 16)
                nc.scalar.activation(gate_sb[:, k // 4, k % 4], gsum_sb[:, k % 2],
                                     ACT.Sigmoid).then_inc(s_gsig, 1)

            def delta(u):
                act.wait_ge(s_zt, u + 1)
                nc.scalar.activation(del_sb[:, bass.ts(u, P)], ps_x[:, 0:P], ACT.Sigmoid,
                                     bias=zbias[:], scale=unscale[:, 1:2]).then_inc(s_del, 1)

            act.wait_ge(s_wready, 1)
            def slot(n, k, v):
                if exists(n + 1):
                    hi(n + 1, k + 1)
                if exists(n - 2):
                    sigmoid_gate(n - 2, (k - 2) % 8, v if k >= 2 else v - 1)
                if k % 4 == 2 and exists(n - 4):
                    delta(v * 2 + k // 4 - 1)
            run_slots(act, -1, TILES + 2, slot)

            for i in range(KT):
                act.wait_ge(s_e_mm, i + 1)
                if i >= 2:
                    act.wait_ge(s_pq, i - 1)
                b = bank[4 * (i % 2):4 * (i % 2) + 4]
                nc.scalar.activation(even_sb[:, i % 2, 0], b[0][:, 0:HALF], ACT.Copy)
                nc.scalar.activation(even_sb[:, i % 2, 1], b[2][:, 0:HALF], ACT.Copy).then_inc(s_even, 1)
            for i in range(KT):
                act.wait_ge(s_u_mm, i + 1)
                act.wait_ge(s_pq, KT)
                if i >= 2:
                    act.wait_ge(s_m, i - 1)
                nc.scalar.activation(even_sb[:, i % 2, 0], bank[2 * (i % 2)][:, 0:HALF], ACT.Copy,
                                     scale=1.0 / D).then_inc(s_u, 1)

            def scan_round(r):
                for s in range(CHUNK):
                    act.wait_ge(s_pre, r * CHUNK + s + 1)
                    nc.scalar.activation(h_sb[:, s::CHUNK], bank[s % 2][:, 0:LANES],
                                         ACT.Tanh).then_inc(s_h, 1)
            scan_round(0)
            scan_round(1)
            act.wait_ge(s_flag, 1)
            changed = act.value_load(flag[0:1, 0:1])
            with act.If(changed > 0):
                with act.Fori(2, BATCH_LANES) as r:
                    scan_round(r)

            def b_hi(n, k):
                act.wait_ge(s_bt, n + 1)
                if before(n, 2):
                    act.wait_ge(s_f, n - 1)
                nc.scalar.activation(hi_sb[:, k % 2], ps_t[k % 2][:], ACT.Copy,
                                     scale=ROW_SCALE).then_inc(s_bhi, 1)

            def squares(n, k):
                act.wait_ge(s_negmu, n + 1)
                nc.scalar.activation(gsum_sb[:, 0], w_sb[:, k % 4], ACT.Square, bias=negmu[:, k % 4:k % 4 + 1],
                                     accum_out=vsum[:, k % 4:k % 4 + 1]).then_inc(s_sq, 1)

            def result(n, k, v):
                act.wait_ge(s_nb2, n + 1)
                if k % 4 == 0 and before(n, 8):
                    act.wait_ge(s_bst[k // 4], v * 16)
                nc.scalar.activation(out_sb[:, k // 4, k % 4], w_sb[:, k % 4], ACT.Identity,
                                     bias=nbias2[:, k % 4:k % 4 + 1],
                                     scale=rstd2[:, k % 4:k % 4 + 1]).then_inc(s_out, 1)

            def slot(n, k, v):
                if exists(n + 1):
                    b_hi(n + 1, k + 1)
                if exists(n - 1):
                    squares(n - 1, (k - 1) % 8)
                if exists(n - 2):
                    result(n - 2, (k - 2) % 8, v if k >= 2 else v - 1)
            run_slots(act, -1, TILES + 1, slot)

        @block.gpsimd
        def _(pool):
            pool.memset(scan_a[:], 0.0).then_inc(s_pool_const, 1)
            pool.memset(c_eps[:], LN_EPS)
            pool.memset(c_eps4[:], LN_EPS / 4)
            pool.memset(c_mean[:], -1.0 / D)
            pool.memset(c_epsd[:], LN_EPS * D)
            pool.memset(c_rootd[:], float(np.sqrt(D)))
            pool.memset(c_half[:], -0.5).then_inc(s_pool_const, 1)
            pool.wait_ge(s_pool_const, 2)
            pool.wait_ge(s_amax, 1)
            pool.partition_all_reduce(amax_all[:, 0:3], amax[:, 0:3], P, ABSMAX).then_inc(s_amax_all, 1)

            def rstd_of(n, k, var_ready, veps_ready, rstd_ready, eps):
                c = slice(k % 4, k % 4 + 1)
                pool.wait_ge(var_ready, n + 1)
                pool.tensor_tensor(veps[:, c], mv[:, k % 4, 1:2], eps[:], ALU.add).then_inc(veps_ready, 1)
                pool.wait_ge(veps_ready, n + 1)
                pool.tensor_tensor(rstd[:, c], veps[:, c], c_half[:], ALU.pow).then_inc(rstd_ready, 1)

            def slot(n, k, v):
                if exists(n + 3):
                    rstd_of(n + 3, (k + 3) % 8, s_aggr, s_veps, s_rstd, c_eps)
            run_slots(pool, -3, TILES - 4, slot)

            pool.wait_ge(s_amax, 2)
            pool.partition_all_reduce(amax_all[:, 3:4], amax[:, 3:4], P, ABSMAX).then_inc(s_amax_all, 1)

            def residual(n, k, v):
                pool.wait_ge(s_gy, n + 1)
                if k % 4 == 0:
                    pool.wait_ge(s_bx[k // 4], v * 16 + 16)
                pool.tensor_tensor(x_sb[:, k // 4, k % 4], x_sb[:, k // 4, k % 4],
                                   gate_sb[:, k // 4, k % 4], ALU.add).then_inc(s_v, 1)

            def add_bias(n, k):
                pool.wait_ge(s_bnorm, n + 1)
                if before(n, 4):
                    pool.wait_ge(s_w, n - 3)
                pool.tensor_tensor(zb_sb[:, k % 4], norm_sb[:, k % 4], fbias_sb[:],
                                   ALU.add).then_inc(s_zb, 1)

            def minus_mean(n, k):
                c = slice(k % 4, k % 4 + 1)
                pool.wait_ge(s_w, n + 1)
                pool.tensor_tensor(negmu[:, c], wsum[:, c], c_mean[:], ALU.mult).then_inc(s_negmu, 1)

            def scale_and_bias(n, k):
                c = slice(k % 4, k % 4 + 1)
                pool.wait_ge(s_sq, n + 1)
                pool.tensor_tensor(var2[:, c], vsum[:, c], c_epsd[:], ALU.add).then_inc(s_var2, 1)
                pool.wait_ge(s_var2, n + 1)
                pool.tensor_tensor(rnorm2[:, c], var2[:, c], c_half[:], ALU.pow).then_inc(s_rnorm2, 1)
                pool.wait_ge(s_rnorm2, n + 1)
                pool.tensor_tensor(rstd2[:, c], rnorm2[:, c], c_rootd[:], ALU.mult).then_inc(s_rstd2, 1)
                pool.wait_ge(s_rstd2, n + 1)
                pool.tensor_tensor(nbias2[:, c], negmu[:, c], rstd2[:, c], ALU.mult).then_inc(s_nb2, 1)

            def slot(n, k, v):
                if exists(n - 1):
                    minus_mean(n - 1, (k - 1) % 8)
                if exists(n + 3):
                    rstd_of(n + 3, (k + 3) % 8, s_baggr, s_bveps, s_brstd, c_eps4)
                if exists(n + 2):
                    add_bias(n + 2, (k + 2) % 8)
                if exists(n - 1):
                    scale_and_bias(n - 1, (k - 1) % 8)
                if exists(n + 4):
                    residual(n + 4, (k + 4) % 8, v if k < 4 else v + 1)
            run_slots(pool, -4, TILES, slot)

        @block.vector
        def _(dve):
            steps = [0]

            def wait_own(instruction):
                steps[0] += 1
                instruction.then_inc(s_dve, 1)
                dve.wait_ge(s_dve, steps[0])

            nc.vector.memset(ones_sb[:], 1.0)
            nc.vector.memset(hd_first[:], 0.0)
            dve.wait_ge(s_wa, 16 * len(WA_LOADS))
            for t in range(KT):
                nc.vector.tensor_copy(wp_rep[:, t].rearrange("p g s -> p g s"),
                                      wp_raw[:, t:t + 1].rearrange("p t a s -> p t (a s)")
                                      .to_broadcast([P, GROUPS, 2 * STATE]))
            for t in range(KT):
                last = nc.vector.tensor_scalar(beta_rep[:, t], ident, 0.0, beta_sb[:, t:t + 1],
                                               ALU.mult, ALU.add)
            last.then_inc(s_brep, 1)
            for t in range(KT):
                nc.vector.tensor_scalar(wg_fold[:, t], wg_raw[:, t], gamma_sb[:, t:t + 1], None, ALU.mult)
                last = nc.vector.tensor_scalar(wp_fold[:, t], wp_raw[:, t].rearrange("p a s -> p (a s)"),
                                               gamma_sb[:, t:t + 1], None, ALU.mult)
            wait_own(last)
            nc.vector.tensor_reduce(amax[:, 0:1], wg_fold[:].rearrange("p t n -> p (t n)"), AX.X,
                                    ALU.max, apply_absolute_value=True)
            nc.vector.tensor_reduce(amax[:, 1:2], wp_fold[:].rearrange("p t n -> p (t n)"), AX.X,
                                    ALU.max, apply_absolute_value=True)
            nc.vector.tensor_reduce(amax[:, 2:3], c_rep[:], AX.X, ALU.max,
                                    apply_absolute_value=True).then_inc(s_amax, 1)

            def scales(a, b):
                wait_own(nc.vector.tensor_scalar(amax_pos[:, a:b], amax_all[:, a:b], 1e-30, None, ALU.max))
                wait_own(nc.vector.tensor_scalar(pow2[:, a:b].bitcast(I32), amax_pos[:, a:b].bitcast(I32),
                                                 0x7F800000, None, ALU.bitwise_and))
                wait_own(nc.vector.reciprocal(pow2_inv[:, a:b], pow2[:, a:b]))
                wait_own(nc.vector.tensor_scalar(unscale[:, a:b], pow2[:, a:b],
                                                 1.0 / (SPLIT_TOP * ROW_SCALE), None, ALU.mult))
                if a == 0:
                    nc.vector.tensor_scalar(unscale[:, 2:3], pow2[:, 2:3],
                                            0.5 / (SPLIT_TOP * STATE_SCALE), None, ALU.mult)
                wait_own(nc.vector.tensor_scalar(scale[:, a:b], pow2_inv[:, a:b], SPLIT_TOP, None, ALU.mult))

            def split(high, low, src, m):
                wait_own(nc.vector.tensor_scalar(high, src, scale[:, m:m + 1], None, ALU.mult))
                wait_own(nc.vector.scalar_tensor_tensor(low, src, scale[:, m:m + 1], high, ALU.mult,
                                                        ALU.subtract))

            dve.wait_ge(s_amax_all, 1)
            scales(0, 3)
            split(wg_hi[:], wg_lo[:], wg_fold[:], 0)
            split(wp_hi[:], wp_lo[:], wp_fold[:], 1)
            split(c_hi[:], c_lo[:], c_rep[:], 2)
            for g in range(GROUPS):
                mask = cst[:, C_MASK + g:C_MASK + g + 1]
                nc.vector.tensor_scalar(cg_hi[:, g], c_hi[:], mask, None, ALU.mult)
                nc.vector.tensor_scalar(cg_lo[:, g], c_lo[:], mask, None, ALU.mult)
            dve.wait_ge(s_bias_mm, 1)
            nc.vector.tensor_tensor(zbias[:], bank[2][:, 0:1], zb_in[:], ALU.add)
            nc.vector.tensor_copy(gbias_sb[:], bank[0][:])
            wait_own(nc.vector.tensor_copy(fbias_sb[:], bank[1][:]))
            nc.vector.sem_inc(s_wready, 1)

            def aggregate(n, k, aggr_done):
                nc.vector.bn_aggr(mv[:, k % 4], bn[:, k % 4]).then_inc(aggr_done, 1)

            def a_statistics(n, k, v):
                if k % 4 == 0:
                    dve.wait_ge(s_xl[k // 4], v * 16 + 16)
                nc.vector.bn_stats(bn[:, k % 4], x_sb[:, k // 4, k % 4]).then_inc(s_bn, 1)

            def a_normalise(n, k):
                dve.wait_ge(s_rstd, n + 1)
                if before(n, 4):
                    dve.wait_ge(s_t, n - 3)
                nc.vector.tensor_scalar(norm_sb[:, k % 4], x_sb[:, k // 4, k % 4], mv[:, k % 4, 0:1],
                                        rstd[:, k % 4:k % 4 + 1], ALU.subtract,
                                        ALU.mult).then_inc(s_norm, 1)

            def low_half(n, k, hi_done, lo_done):
                dve.wait_ge(hi_done, n + 1)
                nc.vector.scalar_tensor_tensor(lo_sb[:, k % 2].rearrange("p t r -> p (t r)"), ps_t[k % 2][:],
                                               ROW_SCALE, hi_sb[:, k % 2].rearrange("p t r -> p (t r)"),
                                               ALU.mult, ALU.subtract).then_inc(lo_done, 1)

            def gate_logits(n, k):
                dve.wait_ge(s_gate, n + 1)
                if before(n, 2):
                    dve.wait_ge(s_gsig, n - 1)
                nc.vector.scalar_tensor_tensor(gsum_sb[:, k % 2], ps_g[k % 2][:], unscale[:, 0:1],
                                               gbias_sb[:], ALU.mult, ALU.add).then_inc(s_gsum, 1)

            def copy_zrow(u, q, v):
                dve.wait_ge(s_proj, (u + 1) * 4)
                if before(u, 1):
                    dve.wait_ge(s_zt, u)
                nc.vector.tensor_copy(zrow[:], ps_z[q % 2][:, 0:P]).then_inc(s_zrow, 1)

            def copy_z(u):
                dve.wait_ge(s_del, u + 1)
                nc.vector.tensor_scalar(z_sb[:, bass.ts(u, P)], ps_x[:, 0:P], unscale[:, 1:2], zbias[:],
                                        ALU.mult, ALU.add).then_inc(s_z, 1)

            def slot(n, k, v):
                if exists(n + 1):
                    low_half(n + 1, k + 1, s_hi, s_lo)
                if k % 4 == 0 and exists(n - 4):
                    copy_zrow(v * 2 + k // 4 - 1, k // 4 + 1, v)
                if k % 4 == 2 and exists(n - 4):
                    copy_z(v * 2 + k // 4 - 1)
                if exists(n - 1):
                    gate_logits(n - 1, (k - 1) % 8)
                if exists(n + 3):
                    a_statistics(n + 3, (k + 3) % 8, v if k < 5 else v + 1)
                if exists(n + 3):
                    dve.wait_ge(s_bn, n + 4)
                if exists(n + 2):
                    a_normalise(n + 2, (k + 2) % 8)
                if exists(n + 3):
                    aggregate(n + 3, (k + 3) % 8, s_aggr)
            run_slots(dve, -3, TILES + 2, slot)

            for i in range(KT):
                dve.wait_ge(s_even, i + 1)
                b = bank[4 * (i % 2):4 * (i % 2) + 4]
                even, odd, even2, odd2 = even_sb[:, i % 2, 0], b[1], even_sb[:, i % 2, 1], b[3]
                nc.vector.tensor_tensor(pt_sb[:, i, 0:HALF], even[:, 0:HALF], odd[:, 0:HALF], ALU.add)
                nc.vector.tensor_tensor(pt_sb[:, i, HALF:D], even[:, HALF - 2:0:-1],
                                        odd[:, HALF - 2:0:-1], ALU.subtract)
                nc.vector.tensor_tensor(qt_sb[:, i, 0:HALF], even2[:, 0:HALF], odd2[:, 0:HALF], ALU.subtract)
                nc.vector.tensor_tensor(qt_sb[:, i, HALF:D], even2[:, HALF - 2:0:-1],
                                        odd2[:, HALF - 2:0:-1], ALU.add).then_inc(s_pq, 1)
            for i in range(KT):
                dve.wait_ge(s_u, i + 1)
                even, odd = even_sb[:, i % 2, 0], bank[2 * (i % 2) + 1]
                nc.vector.scalar_tensor_tensor(m_sb[:, i, 0:HALF], odd[:, 0:HALF], -1.0 / D,
                                               even[:, 0:HALF], ALU.mult, ALU.add)
                nc.vector.scalar_tensor_tensor(m_sb[:, i, HALF:D], odd[:, HALF - 2:0:-1], 1.0 / D,
                                               even[:, HALF - 2:0:-1], ALU.mult, ALU.add).then_inc(s_m, 1)
            dve.wait_ge(s_m, KT)
            nc.vector.tensor_reduce(amax[:, 3:4], m_sb[:].rearrange("p t n -> p (t n)"), AX.X,
                                    ALU.max, apply_absolute_value=True).then_inc(s_amax, 1)
            dve.wait_ge(s_amax_all, 2)
            scales(3, 4)
            split(m_hi, m_lo, m_sb[:], 3)
            nc.vector.sem_inc(s_msplit, 1)

            dve.wait_ge(s_del, QUADS)
            last_step = h_sb[:, CHUNK - 1::CHUNK]

            def scan_round(r, k0):
                if not (isinstance(r, int) and r == 0):
                    dve.wait_ge(s_h, k0)
                    nc.vector.tensor_copy(ends[:], last_step)
                    for b in range(2):
                        a, z = b * BATCH_LANES, (b + 1) * BATCH_LANES
                        last = nc.vector.tensor_tensor(
                            hd_first[:, a + 1:z], h_sb[:, a * CHUNK + CHUNK - 1:(z - 1) * CHUNK:CHUNK],
                            del_sb[:, (a + 1) * CHUNK:z * CHUNK:CHUNK], ALU.mult)
                    last.then_inc(s_hd, 1)
                for s in range(1, CHUNK):
                    dve.wait_ge(s_h, k0 + s)
                    nc.vector.tensor_tensor(hd[:], h_sb[:, s - 1::CHUNK], del_sb[:, s::CHUNK],
                                            ALU.mult).then_inc(s_hd, 1)
                if not (isinstance(r, int) and r == 0):
                    dve.wait_ge(s_h, k0 + CHUNK)

            nc.vector.sem_inc(s_hd, 1)
            scan_round(0, 0)
            scan_round(1, CHUNK)
            nc.vector.tensor_tensor(differ[:], last_step, ends[:], ALU.not_equal).then_inc(s_dscan, 1)
            dve.wait_ge(s_dscan, 1)
            nc.vector.tensor_reduce(n_differ[:], differ[:], AX.X, ALU.add).then_inc(s_cmp, 1)
            dve.wait_ge(s_cnt, 1)
            nc.vector.tensor_copy(flag[:], bank[2][0:1, 0:1]).then_inc(s_flag, 1)
            dve.wait_ge(s_flag, 1)
            changed = dve.value_load(flag[0:1, 0:1])
            with dve.If(changed > 0):
                with dve.Fori(2, BATCH_LANES) as r:
                    scan_round(r, r * CHUNK)
            nc.vector.tensor_scalar(h16[:], h_sb[:], cst[:, C_LOROW:C_LOROW + 1], None,
                                    ALU.mult).then_inc(s_dscan, 1)
            dve.wait_ge(s_dscan, 2)
            nc.vector.scalar_tensor_tensor(h16[:], h_sb[:], STATE_SCALE, h16[:], ALU.mult,
                                           ALU.add).then_inc(s_h16, 1)

            def gated(n, k, v):
                dve.wait_ge(s_y, n + 1)
                if k % 4 == 0:
                    dve.wait_ge(s_bg[k // 4], v * 16 + 16)
                nc.vector.scalar_tensor_tensor(gate_sb[:, k // 4, k % 4], ps_y[k % 2][:], unscale[:, 2:3],
                                               gate_sb[:, k // 4, k % 4], ALU.mult,
                                               ALU.mult).then_inc(s_gy, 1)

            def b_statistics(n, k):
                dve.wait_ge(s_v, n + 1)
                nc.vector.bn_stats(bn[:, k % 4], x_sb[:, k // 4, k % 4]).then_inc(s_bbn, 1)

            def b_normalise(n, k):
                dve.wait_ge(s_brstd, n + 1)
                if before(n, 4):
                    dve.wait_ge(s_bt, n - 3)
                    dve.wait_ge(s_zb, n - 3)
                nc.vector.tensor_scalar(norm_sb[:, k % 4], x_sb[:, k // 4, k % 4], mv[:, k % 4, 0:1],
                                        rstd[:, k % 4:k % 4 + 1], ALU.subtract,
                                        ALU.mult).then_inc(s_bnorm, 1)

            def ffn_sum(n, k):
                dve.wait_ge(s_f, n + 1)
                dve.wait_ge(s_zb, n + 1)
                if before(n, 4):
                    dve.wait_ge(s_out, n - 3)
                nc.vector.scalar_tensor_tensor(w_sb[:, k % 4], ps_g[k % 2][:], unscale[:, 3:4],
                                               zb_sb[:, k % 4], ALU.mult, ALU.add,
                                               accum_out=wsum[:, k % 4:k % 4 + 1]).then_inc(s_w, 1)

            def slot(n, k, v):
                if exists(n + 1):
                    low_half(n + 1, k + 1, s_bhi, s_blo)
                if exists(n - 1):
                    ffn_sum(n - 1, (k - 1) % 8)
                if exists(n + 2):
                    b_normalise(n + 2, (k + 2) % 8)
                if exists(n + 3):
                    b_statistics(n + 3, (k + 3) % 8)
                    dve.wait_ge(s_bbn, n + 4)
                if exists(n + 4):
                    gated(n + 4, (k + 4) % 8, v if k < 4 else v + 1)
                if exists(n + 3):
                    aggregate(n + 3, (k + 3) % 8, s_baggr)
            run_slots(dve, -4, TILES, slot)

        @block.tensor
        def _(pe):
            pe.wait_ge(s_brep, 1)
            for t in range(KT):
                nc.tensor.matmul(bank[0][:], beta_rep[:, t], wg_raw[:, t], start=(t == 0), stop=False)
                nc.tensor.matmul(bank[2][:, 0:1], wp_rep[:, t].rearrange("p g s -> p (g s)"),
                                 beta_sb[:, t:t + 1], start=(t == 0), stop=(t == KT - 1))
            nc.tensor.matmul(bank[0][:], ones_sb[0:1, :], bias_row[0:1, 0, :], start=False, stop=True)
            nc.tensor.matmul(bank[1][:], ones_sb[0:1, :], bias_row[0:1, 1, :], start=True,
                             stop=True).then_inc(s_bias_mm, 1)
            pe.wait_ge(s_wready, 1)

            def transpose(n, k, norm_done, hi_done, lo_done, t_done):
                pe.wait_ge(norm_done, n + 1)
                if before(n, 2):
                    pe.wait_ge(hi_done, n - 1)
                    pe.wait_ge(lo_done, n - 1)
                for t in range(KT):
                    last = nc.tensor.transpose(ps_t[k % 2][:, t * P:(t + 1) * P],
                                               norm_sb[:, k % 4, t * P:(t + 1) * P], ident)
                last.then_inc(t_done, 1)

            def product(dst, k, w_hi, w_lo):
                for t in range(KT):
                    nc.tensor.matmul(dst, hi_sb[:, k % 2, t], w_hi[:, t], start=(t == 0), stop=False)
                    nc.tensor.matmul(dst, hi_sb[:, k % 2, t], w_lo[:, t], start=False, stop=False)
                for t in range(KT):
                    last = nc.tensor.matmul(dst, lo_sb[:, k % 2, t], w_hi[:, t], start=False,
                                            stop=(t == KT - 1))
                return last

            def products(n, k, v):
                pe.wait_ge(s_hi, n + 1)
                pe.wait_ge(s_lo, n + 1)
                if before(n, 2):
                    pe.wait_ge(s_gsum, n - 1)
                product(ps_g[k % 2][:], k, wg_hi, wg_lo).then_inc(s_gate, 1)
                if k % 4 == 0 and before(n, 8):
                    pe.wait_ge(s_zrow, v * 2 + k // 4 - 1)
                g = k % 4
                product(ps_z[k // 4][:, g * 32:(g + 1) * 32], k, wp_hi, wp_lo).then_inc(s_proj, 1)

            def z_transpose(u):
                pe.wait_ge(s_zrow, u + 1)
                if before(u, 1):
                    pe.wait_ge(s_del, u)
                    pe.wait_ge(s_z, u)
                nc.tensor.transpose(ps_x[:, 0:P], zrow[:], ident).then_inc(s_zt, 1)

            def slot(n, k, v):
                if exists(n + 1):
                    transpose(n + 1, k + 1, s_norm, s_hi, s_lo, s_t)
                if k % 4 == 1 and exists(n - 4):
                    z_transpose(v * 2 + k // 4 - 1)
                if exists(n):
                    products(n, k, v)
            run_slots(pe, -1, TILES + 1, slot)

            pe.wait_ge(s_wb, 16 * len(SCAN_A_LOADS + WB_LOADS))
            pe.wait_ge(s_gsum, TILES)
            pe.wait_ge(s_lo, TILES)
            pe.wait_ge(s_zrow, QUADS)
            pe.wait_ge(s_del, QUADS)
            pe.wait_ge(s_z, QUADS)
            for i in range(KT):
                if i >= 2:
                    pe.wait_ge(s_pq, i - 1)
                b = bank[4 * (i % 2):4 * (i % 2) + 4]
                for dst, w, f in ((b[0], w_re_sb, cos_sb), (b[1], w_im_sb, sin_sb),
                                  (b[2], w_im_sb, cos_sb), (b[3], w_re_sb, sin_sb)):
                    for t in range(KT):
                        last = nc.tensor.matmul(dst[:, 0:HALF], w[:, t, i * P:(i + 1) * P], f[:, t],
                                                start=(t == 0), stop=(t == KT - 1))
                last.then_inc(s_e_mm, 1)
            pe.wait_ge(s_pq, KT)
            for i in range(KT):
                if i >= 2:
                    pe.wait_ge(s_m, i - 1)
                b = bank[2 * (i % 2):2 * (i % 2) + 2]
                for dst, w, f in ((b[0], pt_sb, cos_sb), (b[1], qt_sb, sin_sb)):
                    for t in range(KT):
                        last = nc.tensor.matmul(dst[:, 0:HALF], w[:, t, i * P:(i + 1) * P], f[:, t],
                                                start=(t == 0), stop=(t == KT - 1))
                last.then_inc(s_u_mm, 1)
            pe.wait_ge(s_m, KT)

            def scan_round(r, k0):
                def inputs(s):
                    nc.tensor.matmul(bank[s % 2][:, 0:LANES], select, z_sb[:, s::CHUNK],
                                     start=True, stop=False)
                if not (isinstance(r, int) and r == 0):
                    pe.wait_ge(s_h, k0)
                inputs(0)
                for s in range(CHUNK):
                    pe.wait_ge(s_hd, k0 + s + 1)
                    nc.tensor.matmul(bank[s % 2][:, 0:LANES], scan_a[:], (hd if s else hd_first)[:],
                                     start=False, stop=True).then_inc(s_pre, 1)
                    if s + 1 < CHUNK:
                        inputs(s + 1)
            scan_round(0, 0)
            scan_round(1, CHUNK)
            pe.wait_ge(s_cmp, 1)
            nc.tensor.matmul(bank[2][0:1, 0:1], n_differ[:], ones_sb[:, 0:1], start=True,
                             stop=True).then_inc(s_cnt, 1)
            pe.wait_ge(s_flag, 1)
            changed = pe.value_load(flag[0:1, 0:1])
            with pe.If(changed > 0):
                with pe.Fori(2, BATCH_LANES) as r:
                    scan_round(r, r * CHUNK)

            pe.wait_ge(s_h16, 1)
            pe.wait_ge(s_msplit, 1)

            def states_out(n, k, v):
                if before(n, 2):
                    pe.wait_ge(s_gy, n - 1)
                u = v * 2 + k // 4
                g = k % 4
                nc.tensor.matmul(ps_y[k % 2][:], h16[:, bass.ts(u, P)], cg_hi[:, g], start=True, stop=False)
                nc.tensor.matmul(ps_y[k % 2][:], h16[:, bass.ts(u, P)], cg_lo[:, g], start=False,
                                 stop=True).then_inc(s_y, 1)

            def ffn(n, k):
                pe.wait_ge(s_bhi, n + 1)
                pe.wait_ge(s_blo, n + 1)
                if before(n, 2):
                    pe.wait_ge(s_w, n - 1)
                product(ps_g[k % 2][:], k, m_hi, m_lo).then_inc(s_f, 1)

            def slot(n, k, v):
                if exists(n + 1):
                    transpose(n + 1, k + 1, s_bnorm, s_bhi, s_blo, s_bt)
                if exists(n + 4):
                    states_out(n + 4, (k + 4) % 8, v if k < 4 else v + 1)
                if exists(n):
                    ffn(n, k)
            run_slots(pe, -4, TILES - 1, slot)


_INS = ["L0_attn_x", "L0_attn_ln_gamma", "L0_attn_ln_beta", "L0_attn_A", "L0_attn_C", "L0_attn_w_delta",
        "L0_attn_b_delta", "L0_attn_w_in", "L0_attn_b_in", "L0_attn_w_gate", "L0_attn_b_gate",
        "L0_ffn_w_freq_real", "L0_ffn_w_freq_imag", "L0_ffn_bias"]


def shape_constants():
    c = np.zeros((P, C_WIDTH), np.float32)
    c[:, C_IDENT:C_IDENT + P] = np.eye(P)
    for g in range(GROUPS):
        for s in range(STATE):
            k = g * 32 + STATE + s
            c[k, C_SELECT + g * 32 + s] = c[k, C_SELECT + g * 32 + STATE + s] = 1.0
            c[k, C_LOROW] = -STATE_SCALE
        c[g * 32:(g + 1) * 32, C_MASK + g] = 1.0
    return c


def fourier_constants():
    jk = np.outer(np.arange(D), np.arange(HALF)) % D
    a = 2.0 * np.pi * jk / D
    return np.stack([np.cos(a), np.sin(a)]).astype(np.float32)


def kernel(**inputs):
    import concourse.bacc as _bacc
    from concourse.bass_utils import run_bass_kernel_spmd as _run

    nc = _bacc.Bacc("TRN2", target_bir_lowering=False, num_devices=1)
    arrays = {name: np.ascontiguousarray(inputs[name]) for name in _INS}
    arrays["L0_attn_x"] = arrays["L0_attn_x"].reshape(BATCH * SEQ, D)
    for name in ("L0_attn_ln_gamma", "L0_attn_ln_beta"):
        arrays[name] = np.ascontiguousarray(arrays[name].reshape(KT, P).T)
    arrays["shape_constants"] = shape_constants()
    arrays["fourier_constants"] = fourier_constants()
    args = [nc.dram_tensor(k, a.shape, mybir.dt.from_np(a.dtype), kind="ExternalInput").ap()
            for k, a in arrays.items()]
    out = nc.dram_tensor("out", (BATCH * SEQ, D), F32, kind="ExternalOutput").ap()
    gate_dram = nc.dram_tensor("gate_dram", (BATCH * SEQ, D), F32, kind="Internal").ap()
    build(nc, *args, out, gate_dram)
    r = _run(nc, [arrays], core_ids=[0])
    return r.results[0]["out"].reshape(BATCH, SEQ, D)
```

```python
from contextlib import ExitStack

import numpy as np

import concourse.bass as bass
from concourse import mybir

P = 128
BATCH, SEQ, D = 8, 2048, 512
STATE = 16
KT = D // P
GROUPS = 4
GROUP_ROWS = BATCH * SEQ // GROUPS
QUADS = GROUP_ROWS // P
TILES = QUADS * GROUPS
OCTETS = TILES // 8
HALF = D // 2 + 1
CHUNK = 16
LANES = GROUP_ROWS // CHUNK
BATCH_LANES = SEQ // CHUNK
LN_EPS = 1e-5
SPLIT_TOP = 2.0 ** 14
ROW_SCALE = 2.0 ** 11
STATE_SCALE = 2.0 ** 14

ALU = mybir.AluOpType
ACT = mybir.ActivationFunctionType
F32 = mybir.dt.float32
F16 = mybir.dt.float16
BF16 = mybir.dt.bfloat16
I32 = mybir.dt.int32
AX = mybir.AxisListType
ABSMAX = bass.bass_isa.ReduceOp.absmax

C_IDENT, C_SELECT = 0, P
C_LOW_STATE = 2 * P
C_LOW_C = C_LOW_STATE + 1
C_GROUP = C_LOW_C + 1
C_PART = C_GROUP + 2
C_WIDTH = C_PART + 3
STEPS = 2 * CHUNK
PAIRS = 3 * KT


def exists(n):
    return not isinstance(n, int) or 0 <= n < TILES


def before(n, k):
    return not isinstance(n, int) or n >= k


def run_slots(engine, first, last, slot):
    for n in range(first, 8):
        slot(n, n % 8, n // 8)
    with engine.Fori(1, OCTETS - 1) as v:
        for k in range(8):
            slot(v * 8 + k, k, v)
    for n in range(TILES - 8, last + 1):
        slot(n, n % 8, n // 8)


def build(nc, x, gamma, beta, A, C, w_delta, b_delta, w_in, b_in, w_gate, b_gate, w_re, w_im,
          ffn_bias, consts, dft, out, gate_dram):
    ctx = ExitStack()
    with ctx:
        def sb(name, shape, dt=F32):
            return ctx.enter_context(nc.sbuf_tensor(name, shape, dt))

        def sem(name):
            return ctx.enter_context(nc.semaphore(name))

        x_sb = sb("x_sb", [P, 2, GROUPS, D])
        gate_sb = sb("gate_sb", [P, 2, GROUPS, D])
        out_sb = sb("out_sb", [P, 2, GROUPS, D])
        norm_sb = sb("norm_sb", [P, 4, D])
        hi_sb = sb("hi_sb", [P, 2, KT, P], F16)
        lo_sb = sb("lo_sb", [P, 2, KT, P], F16)
        gsum_sb = sb("gsum_sb", [P, 2, D])
        w_ring = sb("w_ring", [P, 2 * KT, D])
        wg_raw, wg_fold = w_ring[:, 0:KT], w_ring[:, KT:2 * KT]
        m_sb = wg_fold
        wg_hi = sb("wg_hi", [P, KT, D], F16)
        wg_lo = sb("wg_lo", [P, KT, D], F16)
        wp_raw = sb("wp_raw", [P, KT, 2, STATE])
        wp_rep = sb("wp_rep", [P, KT, GROUPS, 2 * STATE])
        wp_fold = sb("wp_fold", [P, KT, 2 * STATE])
        wp_hi = sb("wp_hi", [P, KT, 2 * STATE], F16)
        wp_lo = sb("wp_lo", [P, KT, 2 * STATE], F16)
        gamma_sb = sb("gamma_sb", [P, KT])
        beta_sb = sb("beta_sb", [P, KT])
        beta_rep = sb("beta_rep", [P, KT, P])
        bias_row = sb("bias_row", [1, 2, D])
        ones_sb = sb("ones_sb", [P, P])
        gbias_sb = sb("gbias_sb", [P, D])
        fbias_sb = sb("fbias_sb", [P, D])
        fb_part = [sb(f"fb_part{i}", [P, D], BF16) for i in range(3)]
        fb_rows = sb("fb_rows", [P, D], BF16)
        fb_ones = sb("fb_ones", [P, P], BF16)
        zb_in = sb("zb_in", [P, 1])
        zbias = sb("zbias", [P, 1])
        cst = sb("cst", [P, C_WIDTH])
        ident = cst[:, C_IDENT:C_IDENT + P]
        select = cst[:, C_SELECT:C_SELECT + P]
        scan_a = sb("scan_a", [P, P])
        c_rep = sb("c_rep", [P, D])
        c_both = sb("c_both", [P, D], F16)
        c_parts = sb("c_parts", [P, 2, D], F16)
        amax = sb("amax", [P, 4])
        amax_all = sb("amax_all", [P, 4])
        amax_pos = sb("amax_pos", [P, 4])
        pow2 = sb("pow2", [P, 4])
        pow2_inv = sb("pow2_inv", [P, 4])
        scale = sb("scale", [P, 4])
        unscale = sb("unscale", [P, 4])
        zrow = sb("zrow", [P, P])
        z_sb = sb("z_sb", [P, GROUP_ROWS])
        del_sb = sb("del_sb", [P, GROUP_ROWS])
        h_sb = sb("h_sb", [P, GROUP_ROWS])
        h16 = sb("h16", [P, GROUP_ROWS], F16)
        h_rep = [z_sb[:].bitcast(F16)[:, i * GROUP_ROWS:(i + 1) * GROUP_ROWS] for i in range(2)]
        hd = sb("hd", [P, LANES])
        hd_first = sb("hd_first", [P, LANES])
        ends = sb("ends", [P, LANES])
        differ = sb("differ", [P, LANES])
        n_differ = sb("n_differ", [P, 1])
        flag = sb("flag", [1, 1], I32)
        w_re_sb = sb("w_re_sb", [P, KT, D])
        w_im_sb = sb("w_im_sb", [P, KT, D])
        cos_sb = sb("cos_sb", [P, KT, HALF])
        sin_sb = sb("sin_sb", [P, KT, HALF])
        even_sb = sb("even_sb", [P, 2, HALF])
        m_amax = sb("m_amax", [P, KT])
        pt_sb = out_sb[:, 0]
        qt_sb = out_sb[:, 1]
        m_split = w_re_sb[:].bitcast(F16)
        m_hi, m_lo = m_split[:, :, 0:D], m_split[:, :, D:2 * D]
        bn = sb("bn", [P, 4, 6])
        mv = sb("mv", [P, 4, 2])
        veps = sb("veps", [P, 4])
        rstd = sb("rstd", [P, 4])
        c_eps = sb("c_eps", [P, 1])
        c_eps4 = sb("c_eps4", [P, 1])
        c_half = sb("c_half", [P, 2])
        wsum = sb("wsum", [P, 8])
        negmu = sb("negmu", [P, 8])
        vsum = sb("vsum", [P, 8])
        var2 = sb("var2", [P, 8])
        rnorm2 = sb("rnorm2", [P, 8])
        rstd2 = sb("rstd2", [P, 8])
        c_mean = sb("c_mean", [P, 1])
        c_epsd = sb("c_epsd", [P, 2])
        c_rootd = sb("c_rootd", [P, 2])
        nbias2 = sb("nbias2", [P, 8])

        bank = [ctx.enter_context(nc.psum_tensor(f"bank{i}", [P, 512], F32)) for i in range(8)]
        ps_t, ps_g, ps_z, ps_x, ps_y = bank[0:2], bank[2:4], bank[4:6], bank[6], bank[4:6]

        def tiles_of(t):
            return t.rearrange("(g u p) d -> u p g d", g=GROUPS, p=P)

        x_v, out_v, gate_v = tiles_of(x), tiles_of(out), tiles_of(gate_dram)

        s_wa = sem("weights_loaded")
        s_wb = sem("fourier_loaded")
        s_pool_const = sem("pool_constants")
        s_dve = sem("dve_step")
        s_amax = sem("amax_ready")
        s_amax_all = sem("amax_reduced")
        s_brep = sem("beta_replicated")
        s_bias_mm = sem("bias_products")
        s_wready = sem("weights_split")
        s_xl = [sem(f"x_loaded{i}") for i in range(2)]
        s_gst = [sem(f"gate_stored{i}") for i in range(2)]
        s_bn = sem("a_bn")
        s_aggr = sem("a_variance")
        s_veps = sem("a_variance_eps")
        s_rstd = sem("a_rstd")
        s_norm = sem("a_norm")
        s_t = sem("a_transposed")
        s_hi = sem("a_hi")
        s_lo = sem("a_lo")
        s_gate = sem("a_gate_products")
        s_proj = sem("a_projections")
        s_gsum = sem("a_gate_logits")
        s_gsig = sem("a_gate")
        s_zrow = sem("a_zrow")
        s_zt = sem("a_z_transposed")
        s_del = sem("a_delta")
        s_z = sem("a_z")
        s_mm = sem("m_products")
        s_even = sem("m_even_copied")
        s_pair = sem("m_pair_combined")
        s_msplit = sem("m_split")
        s_low = sem("scan_low_half")
        s_fb = sem("ffn_bias_parts")
        s_hrep = sem("h_rep_loaded")
        s_hd = sem("scan_hd")
        s_pre = sem("scan_pre")
        s_h = sem("scan_h")
        s_cmp = sem("scan_compared")
        s_cnt = sem("scan_counted")
        s_flag = sem("scan_flag")
        s_dscan = sem("scan_dve")
        s_split = sem("scan_split")
        s_mamax = sem("m_maxima")
        s_h16 = sem("h16_ready")
        s_bx = [sem(f"b_x_loaded{i}") for i in range(2)]
        s_bg = [sem(f"b_gate_loaded{i}") for i in range(2)]
        s_bst = [sem(f"b_stored{i}") for i in range(2)]
        s_y = sem("b_y")
        s_gy = sem("b_gated")
        s_v = sem("b_v")
        s_bbn = sem("b_bn")
        s_baggr = sem("b_variance")
        s_bveps = sem("b_variance_eps")
        s_brstd = sem("b_rstd")
        s_bnorm = sem("b_norm")
        s_bt = sem("b_transposed")
        s_bhi = sem("b_hi")
        s_blo = sem("b_lo")
        s_f = sem("b_ffn_products")
        s_w = sem("b_w")
        s_negmu = sem("b_negmu")
        s_sq = sem("b_squares")
        s_var2 = sem("b_var2")
        s_rnorm2 = sem("b_rnorm2")
        s_rstd2 = sem("b_rstd2")
        s_nb2 = sem("b_nbias2")
        s_out = sem("b_out")

        H_PIECES = [(0, 2 * P), (2 * P, GROUP_ROWS)]

        def on_scan_step(k):
            return k if k < 4 * KT else k - 1 if 4 * KT < k <= 2 * PAIRS else None

        def pair_copied(k):
            j = on_scan_step(k)
            return j // 2 if j is not None and j % 2 else None

        def pair_combined(k):
            return pair_copied(k - 1) if k else None

        block = ctx.enter_context(nc.Block())

        @block.sync
        def _(sp):
            def load_x(u, par, loaded):
                sp.dma_start(x_sb[:, par], x_v[u]).then_inc(loaded[par], 16)

            def first_pass(u, par, v):
                if not isinstance(u, int) or u + 2 < QUADS:
                    sp.wait_ge(s_norm, (u + 1) * 4)
                    load_x(u + 2, par, s_xl)
                sp.wait_ge(s_gsig, (u + 1) * 4)
                sp.dma_start(gate_v[u], gate_sb[:, par]).then_inc(s_gst[par], 16)

            load_x(0, 0, s_xl)
            load_x(1, 1, s_xl)
            with sp.Fori(0, OCTETS - 1) as v:
                first_pass(v * 2, 0, v)
                first_pass(v * 2 + 1, 1, v)
            first_pass(QUADS - 2, 0, OCTETS - 1)
            first_pass(QUADS - 1, 1, OCTETS - 1)

            def load_gate(u, par):
                sp.dma_start(gate_sb[:, par], gate_v[u]).then_inc(s_bg[par], 16)

            def store_result(u, par):
                sp.wait_ge(s_out, u * 4 + 4)
                sp.dma_start(out_v[u], out_sb[:, par]).then_inc(s_bst[par], 16)

            def second_pass(u, par, first=False):
                if not isinstance(u, int) or u + 2 < QUADS:
                    sp.wait_ge(s_v, u * 4 + 4)
                    load_gate(u + 2, par)
                if not first:
                    store_result(u - 2, par)
                if not isinstance(u, int) or u + 2 < QUADS:
                    sp.wait_ge(s_bnorm, u * 4 + 4)
                    load_x(u + 2, par, s_bx)

            sp.wait_ge(s_norm, TILES)
            sp.wait_ge(s_gst[0], 16 * OCTETS)
            sp.wait_ge(s_gst[1], 16 * OCTETS)
            for u in range(2):
                load_x(u, u, s_bx)
                load_gate(u, u)
            sp.wait_ge(s_h16, 1)
            for a, z in H_PIECES:
                for i in range(2):
                    for r in range(2):
                        sp.dma_start(h_rep[i][r * 64:(r + 1) * 64, a:z],
                                     h16[i * 64:(i + 1) * 64, a:z]).then_inc(s_hrep, 16)
                if a == 0:
                    sp.wait_ge(s_hrep, 4 * 16)
            second_pass(0, 0, first=True)
            second_pass(1, 1, first=True)
            with sp.Fori(1, OCTETS - 1) as v:
                second_pass(v * 2, 0)
                second_pass(v * 2 + 1, 1)
            second_pass(QUADS - 2, 0)
            second_pass(QUADS - 1, 1)
            store_result(QUADS - 2, 0)
            store_result(QUADS - 1, 1)
            sp.wait_ge(s_bst[0], 16 * OCTETS)
            sp.wait_ge(s_bst[1], 16 * OCTETS)

        WA_LOADS = [
            (wg_raw, w_gate.rearrange("(t p) n -> p t n", p=P)),
            (wp_raw[:, :, 0, :], w_delta.rearrange("(t p) n -> p t n", p=P)),
            (wp_raw[:, :, 1, :], w_in.rearrange("(t p) n -> p t n", p=P)),
            (gamma_sb[:], gamma),
            (beta_sb[:], beta),
            (bias_row[0:1, 0, :], b_gate.rearrange("(a n) -> a n", a=1)),
            (bias_row[0:1, 1, :], ffn_bias.rearrange("(a n) -> a n", a=1)),
            (cst[:], consts),
        ]
        for g in range(GROUPS):
            p0, p1 = g * 2 * STATE, g * 2 * STATE + STATE
            WA_LOADS += [
                (zb_in[p0:p0 + STATE, :], b_delta.rearrange("(n a) -> n a", a=1)),
                (zb_in[p1:p1 + STATE, :], b_in.rearrange("(n a) -> n a", a=1)),
                (c_rep[p0:p0 + STATE, :], C),
                (c_rep[p1:p1 + STATE, :], C),
            ]
        SCAN_A_LOADS = [(scan_a[g * 32:g * 32 + STATE, g * 32 + r * STATE:g * 32 + (r + 1) * STATE], A)
                        for g in range(GROUPS) for r in range(2)]
        WB_LOADS = [
            (w_re_sb[:], w_re.rearrange("(t p) n -> p t n", p=P)),
            (w_im_sb[:], w_im.rearrange("(t p) n -> p t n", p=P)),
            (cos_sb[:], dft[0].rearrange("(t p) n -> p t n", p=P)),
            (sin_sb[:], dft[1].rearrange("(t p) n -> p t n", p=P)),
        ]

        @block.scalar
        def _(act):
            for dst, src in WA_LOADS:
                act.dma_start(dst, src).then_inc(s_wa, 16)
            act.wait_ge(s_pool_const, 1)
            for dst, src in SCAN_A_LOADS + WB_LOADS:
                act.dma_start(dst, src).then_inc(s_wb, 16)

            def hi(n, k):
                act.wait_ge(s_t, n + 1)
                if before(n, 2):
                    act.wait_ge(s_proj, n - 1)
                nc.scalar.activation(hi_sb[:, k % 2], ps_t[k % 2][:], ACT.Copy,
                                     scale=ROW_SCALE).then_inc(s_hi, 1)

            def sigmoid_gate(n, k, v):
                act.wait_ge(s_gsum, n + 1)
                if k % 4 == 0 and before(n, 8):
                    act.wait_ge(s_gst[k // 4], v * 16)
                nc.scalar.activation(gate_sb[:, k // 4, k % 4], gsum_sb[:, k % 2],
                                     ACT.Sigmoid).then_inc(s_gsig, 1)

            def delta(u):
                act.wait_ge(s_zt, u + 1)
                nc.scalar.activation(del_sb[:, bass.ts(u, P)], ps_x[:, 0:P], ACT.Sigmoid,
                                     bias=zbias[:], scale=unscale[:, 1:2]).then_inc(s_del, 1)

            act.wait_ge(s_wready, 1)
            def slot(n, k, v):
                if exists(n + 1):
                    hi(n + 1, k + 1)
                if exists(n - 2):
                    sigmoid_gate(n - 2, (k - 2) % 8, v if k >= 2 else v - 1)
                if k % 4 == 2 and exists(n - 4):
                    delta(v * 2 + k // 4 - 1)
            run_slots(act, -1, TILES + 2, slot)

            def copy_even(q):
                act.wait_ge(s_mm, 2 * q + 1)
                if q >= 2:
                    act.wait_ge(s_pair, q - 1)
                nc.scalar.activation(even_sb[:, q % 2], bank[2 + 2 * (q % 2)][:, 0:HALF], ACT.Copy,
                                     scale=1.0 if q < 2 * KT else 1.0 / D).then_inc(s_even, 1)

            def scan_round(r, k0, lows0):
                for s in range(CHUNK):
                    act.wait_ge(s_pre, k0 + s + 1)
                    nc.scalar.activation(h_sb[:, s::CHUNK], bank[s % 2][:, 0:LANES],
                                         ACT.Tanh).then_inc(s_h, 1)
                    if isinstance(r, int) and pair_copied(k0 + s) is not None:
                        copy_even(pair_copied(k0 + s))
                    if lows0 is not None:
                        act.wait_ge(s_h, k0 + s + 1)
                        nc.scalar.activation(h16[:, s::CHUNK], h_sb[:, s::CHUNK], ACT.Copy,
                                             scale=cst[:, C_LOW_STATE:C_LOW_STATE + 1]).then_inc(s_low, 1)
            scan_round(0, 0, None)
            scan_round(1, CHUNK, 0)
            act.wait_ge(s_flag, 1)
            changed = act.value_load(flag[0:1, 0:1])
            with act.If(changed > 0):
                with act.Fori(2, BATCH_LANES) as r:
                    scan_round(r, r * CHUNK, (r - 1) * CHUNK)

            def b_hi(n, k):
                act.wait_ge(s_bt, n + 1)
                if before(n, 2):
                    act.wait_ge(s_f, n - 1)
                nc.scalar.activation(hi_sb[:, k % 2], ps_t[k % 2][:], ACT.Copy,
                                     scale=ROW_SCALE).then_inc(s_bhi, 1)

            def squares(n, k):
                act.wait_ge(s_negmu, n + 1)
                if before(n, 2):
                    act.wait_ge(s_sq, n - 1)
                nc.scalar.activation(gsum_sb[:, k % 2], w_ring[:, k], ACT.Square, bias=negmu[:, k:k + 1],
                                     accum_out=vsum[:, k:k + 1]).then_inc(s_sq, 1)

            def result(n, k, v):
                act.wait_ge(s_nb2, v * 4 + k // 2 + 1)
                if k % 4 == 0 and before(n, 8):
                    act.wait_ge(s_bst[k // 4], v * 16)
                nc.scalar.activation(out_sb[:, k // 4, k % 4], w_ring[:, k], ACT.Identity,
                                     bias=nbias2[:, k:k + 1], scale=rstd2[:, k:k + 1]).then_inc(s_out, 1)

            def slot(n, k, v):
                if exists(n + 1):
                    b_hi(n + 1, k + 1)
                if exists(n - 5):
                    result(n - 5, (k - 5) % 8, v if k >= 5 else v - 1)
                if exists(n - 2):
                    squares(n - 2, (k - 2) % 8)
            run_slots(act, -1, TILES + 4, slot)

        @block.gpsimd
        def _(pool):
            pool.memset(scan_a[:], 0.0).then_inc(s_pool_const, 1)
            pool.memset(c_eps[:], LN_EPS)
            pool.memset(c_eps4[:], LN_EPS / 4)
            pool.memset(c_mean[:], -1.0 / D)
            pool.memset(c_epsd[:], LN_EPS * D)
            pool.memset(c_rootd[:], float(np.sqrt(D)))
            pool.memset(c_half[:], -0.5).then_inc(s_pool_const, 1)
            pool.wait_ge(s_pool_const, 2)
            pool.wait_ge(s_amax, 1)
            pool.partition_all_reduce(amax_all[:, 0:3], amax[:, 0:3], P, ABSMAX).then_inc(s_amax_all, 1)

            def rstd_of(n, k, var_ready, veps_ready, rstd_ready, eps):
                c = slice(k % 4, k % 4 + 1)
                pool.wait_ge(var_ready, n + 1)
                pool.tensor_tensor(veps[:, c], mv[:, k % 4, 1:2], eps[:], ALU.add).then_inc(veps_ready, 1)
                pool.wait_ge(veps_ready, n + 1)
                pool.tensor_tensor(rstd[:, c], veps[:, c], c_half[:, 0:1], ALU.pow).then_inc(rstd_ready, 1)

            def slot(n, k, v):
                if exists(n + 3):
                    rstd_of(n + 3, (k + 3) % 8, s_aggr, s_veps, s_rstd, c_eps)
            run_slots(pool, -3, TILES - 4, slot)

            pool.wait_ge(s_amax, 2)
            pool.partition_all_reduce(amax_all[:, 3:4], amax[:, 3:4], P, ABSMAX).then_inc(s_amax_all, 1)

            def residual(n, k, v):
                pool.wait_ge(s_gy, n + 1)
                if k % 4 == 0:
                    pool.wait_ge(s_bx[k // 4], v * 16 + 16)
                pool.tensor_tensor(x_sb[:, k // 4, k % 4], x_sb[:, k // 4, k % 4],
                                   gate_sb[:, k // 4, k % 4], ALU.add).then_inc(s_v, 1)

            def minus_mean(n, k):
                pool.wait_ge(s_w, n + 1)
                pool.tensor_tensor(negmu[:, k:k + 1], wsum[:, k:k + 1], c_mean[:],
                                   ALU.mult).then_inc(s_negmu, 1)

            def scale_and_bias(m, k):
                c = slice(k, k + 2)
                pool.wait_ge(s_sq, m * 2 + 2)
                pool.tensor_tensor(var2[:, c], vsum[:, c], c_epsd[:], ALU.add).then_inc(s_var2, 1)
                pool.wait_ge(s_var2, m + 1)
                pool.tensor_tensor(rnorm2[:, c], var2[:, c], c_half[:], ALU.pow).then_inc(s_rnorm2, 1)
                pool.wait_ge(s_rnorm2, m + 1)
                pool.tensor_tensor(rstd2[:, c], rnorm2[:, c], c_rootd[:], ALU.mult).then_inc(s_rstd2, 1)
                pool.wait_ge(s_rstd2, m + 1)
                pool.tensor_tensor(nbias2[:, c], negmu[:, c], rstd2[:, c], ALU.mult).then_inc(s_nb2, 1)

            def slot(n, k, v):
                if exists(n + 3):
                    rstd_of(n + 3, (k + 3) % 8, s_baggr, s_bveps, s_brstd, c_eps4)
                if exists(n - 2):
                    minus_mean(n - 2, (k - 2) % 8)
                if exists(n + 5):
                    residual(n + 5, (k + 5) % 8, v if k < 3 else v + 1)
                if k % 2 == 0 and exists(n - 4):
                    scale_and_bias(v * 4 + k // 2 - 2, (k - 4) % 8)
            run_slots(pool, -5, TILES + 2, slot)

        @block.vector
        def _(dve):
            steps = [0]

            def wait_own(instruction):
                steps[0] += 1
                instruction.then_inc(s_dve, 1)
                dve.wait_ge(s_dve, steps[0])

            nc.vector.memset(ones_sb[:], 1.0)
            nc.vector.memset(hd_first[:], 0.0)
            dve.wait_ge(s_wa, 16 * len(WA_LOADS))
            for t in range(KT):
                nc.vector.tensor_copy(wp_rep[:, t].rearrange("p g s -> p g s"),
                                      wp_raw[:, t:t + 1].rearrange("p t a s -> p t (a s)")
                                      .to_broadcast([P, GROUPS, 2 * STATE]))
            for t in range(KT):
                last = nc.vector.tensor_scalar(beta_rep[:, t], ident, 0.0, beta_sb[:, t:t + 1],
                                               ALU.mult, ALU.add)
            last.then_inc(s_brep, 1)
            for t in range(KT):
                nc.vector.tensor_scalar(wg_fold[:, t], wg_raw[:, t], gamma_sb[:, t:t + 1], None, ALU.mult)
                last = nc.vector.tensor_scalar(wp_fold[:, t], wp_raw[:, t].rearrange("p a s -> p (a s)"),
                                               gamma_sb[:, t:t + 1], None, ALU.mult)
            wait_own(last)
            nc.vector.tensor_reduce(amax[:, 0:1], wg_fold.rearrange("p t n -> p (t n)"), AX.X,
                                    ALU.max, apply_absolute_value=True)
            nc.vector.tensor_reduce(amax[:, 1:2], wp_fold[:].rearrange("p t n -> p (t n)"), AX.X,
                                    ALU.max, apply_absolute_value=True)
            nc.vector.tensor_reduce(amax[:, 2:3], c_rep[:], AX.X, ALU.max,
                                    apply_absolute_value=True).then_inc(s_amax, 1)

            def scales(a, b):
                wait_own(nc.vector.tensor_scalar(amax_pos[:, a:b], amax_all[:, a:b], 1e-30, None, ALU.max))
                wait_own(nc.vector.tensor_scalar(pow2[:, a:b].bitcast(I32), amax_pos[:, a:b].bitcast(I32),
                                                 0x7F800000, None, ALU.bitwise_and))
                wait_own(nc.vector.reciprocal(pow2_inv[:, a:b], pow2[:, a:b]))
                wait_own(nc.vector.tensor_scalar(unscale[:, a:b], pow2[:, a:b],
                                                 1.0 / (SPLIT_TOP * ROW_SCALE), None, ALU.mult))
                if a == 0:
                    nc.vector.tensor_scalar(unscale[:, 2:3], pow2[:, 2:3],
                                            0.5 / (SPLIT_TOP * STATE_SCALE), None, ALU.mult)
                wait_own(nc.vector.tensor_scalar(scale[:, a:b], pow2_inv[:, a:b], SPLIT_TOP, None, ALU.mult))

            def split(high, low, src, m):
                wait_own(nc.vector.tensor_scalar(high, src, scale[:, m:m + 1], None, ALU.mult))
                wait_own(nc.vector.scalar_tensor_tensor(low, src, scale[:, m:m + 1], high, ALU.mult,
                                                        ALU.subtract))

            dve.wait_ge(s_amax_all, 1)
            scales(0, 3)
            split(wg_hi[:], wg_lo[:], wg_fold, 0)
            split(wp_hi[:], wp_lo[:], wp_fold[:], 1)
            wait_own(nc.vector.tensor_scalar(c_both[:], c_rep[:], scale[:, 2:3],
                                             cst[:, C_LOW_C:C_LOW_C + 1], ALU.mult, ALU.mult))
            wait_own(nc.vector.scalar_tensor_tensor(c_both[:], c_rep[:], scale[:, 2:3], c_both[:],
                                                    ALU.mult, ALU.add))
            for j in range(2):
                nc.vector.tensor_scalar(c_parts[:, j], c_both[:], cst[:, C_GROUP + j:C_GROUP + j + 1],
                                        None, ALU.mult)
            dve.wait_ge(s_bias_mm, 1)
            nc.vector.tensor_tensor(zbias[:], bank[2][:, 0:1], zb_in[:], ALU.add)
            nc.vector.tensor_copy(gbias_sb[:], bank[0][:])
            wait_own(nc.vector.tensor_copy(fbias_sb[:], bank[1][:]))
            nc.vector.sem_inc(s_wready, 1)

            def aggregate(n, k, aggr_done):
                nc.vector.bn_aggr(mv[:, k % 4], bn[:, k % 4]).then_inc(aggr_done, 1)

            def a_statistics(n, k, v):
                if k % 4 == 0:
                    dve.wait_ge(s_xl[k // 4], v * 16 + 16)
                nc.vector.bn_stats(bn[:, k % 4], x_sb[:, k // 4, k % 4]).then_inc(s_bn, 1)

            def a_normalise(n, k):
                dve.wait_ge(s_rstd, n + 1)
                if before(n, 4):
                    dve.wait_ge(s_t, n - 3)
                nc.vector.tensor_scalar(norm_sb[:, k % 4], x_sb[:, k // 4, k % 4], mv[:, k % 4, 0:1],
                                        rstd[:, k % 4:k % 4 + 1], ALU.subtract,
                                        ALU.mult).then_inc(s_norm, 1)

            def low_half(n, k, hi_done, lo_done):
                dve.wait_ge(hi_done, n + 1)
                nc.vector.scalar_tensor_tensor(lo_sb[:, k % 2].rearrange("p t r -> p (t r)"), ps_t[k % 2][:],
                                               ROW_SCALE, hi_sb[:, k % 2].rearrange("p t r -> p (t r)"),
                                               ALU.mult, ALU.subtract).then_inc(lo_done, 1)

            def gate_logits(n, k):
                dve.wait_ge(s_gate, n + 1)
                if before(n, 2):
                    dve.wait_ge(s_gsig, n - 1)
                nc.vector.scalar_tensor_tensor(gsum_sb[:, k % 2], ps_g[k % 2][:], unscale[:, 0:1],
                                               gbias_sb[:], ALU.mult, ALU.add).then_inc(s_gsum, 1)

            def copy_zrow(u, q, v):
                dve.wait_ge(s_proj, (u + 1) * 4)
                if before(u, 1):
                    dve.wait_ge(s_zt, u)
                nc.vector.tensor_copy(zrow[:], ps_z[q % 2][:, 0:P]).then_inc(s_zrow, 1)

            def copy_z(u):
                dve.wait_ge(s_del, u + 1)
                nc.vector.tensor_scalar(z_sb[:, bass.ts(u, P)], ps_x[:, 0:P], unscale[:, 1:2], zbias[:],
                                        ALU.mult, ALU.add).then_inc(s_z, 1)

            def slot(n, k, v):
                if k % 4 == 3 and exists(n - 7):
                    copy_z(v * 2 + k // 4 - 1)
                if exists(n + 3):
                    a_statistics(n + 3, (k + 3) % 8, v if k < 5 else v + 1)
                if exists(n + 3):
                    dve.wait_ge(s_bn, n + 4)
                if exists(n + 2):
                    a_normalise(n + 2, (k + 2) % 8)
                if exists(n + 3):
                    aggregate(n + 3, (k + 3) % 8, s_aggr)
                if exists(n + 1):
                    low_half(n + 1, k + 1, s_hi, s_lo)
                if exists(n - 1):
                    gate_logits(n - 1, (k - 1) % 8)
                if k % 4 == 0 and exists(n - 4):
                    copy_zrow(v * 2 + k // 4 - 1, k // 4 + 1, v)
            run_slots(dve, -3, TILES + 3, slot)

            def combine(q):
                dve.wait_ge(s_mm, 2 * q + 2)
                dve.wait_ge(s_even, q + 1)
                even, odd, i = even_sb[:, q % 2], bank[3 + 2 * (q % 2)], q // 2
                if q < 2 * KT:
                    dst = (pt_sb, qt_sb)[q % 2][:, i]
                    front, mirrored = (ALU.add, ALU.subtract) if q % 2 == 0 else (ALU.subtract, ALU.add)
                    nc.vector.tensor_tensor(dst[:, 0:HALF], even, odd[:, 0:HALF], front)
                    nc.vector.tensor_tensor(dst[:, HALF:D], even[:, HALF - 2:0:-1],
                                            odd[:, HALF - 2:0:-1], mirrored).then_inc(s_pair, 1)
                else:
                    i = q - 2 * KT
                    nc.vector.scalar_tensor_tensor(m_sb[:, i, 0:HALF], odd[:, 0:HALF], -1.0 / D, even,
                                                   ALU.mult, ALU.add)
                    nc.vector.scalar_tensor_tensor(m_sb[:, i, HALF:D], odd[:, HALF - 2:0:-1], 1.0 / D,
                                                   even[:, HALF - 2:0:-1], ALU.mult,
                                                   ALU.add).then_inc(s_pair, 1)

            def bias_part(i):
                wait_own(nc.vector.tensor_copy(fb_part[i][:], fbias_sb[:]))
                if i < 2:
                    wait_own(nc.vector.tensor_tensor(fbias_sb[:], fbias_sb[:], fb_part[i][:], ALU.subtract))

            def bias_row_of(i):
                row = cst[:, C_PART + i:C_PART + i + 1]
                if i == 0:
                    wait_own(nc.vector.tensor_scalar(fb_rows[:], fb_part[0][:], row, None, ALU.mult))
                else:
                    wait_own(nc.vector.scalar_tensor_tensor(fb_rows[:], fb_part[i][:], row, fb_rows[:],
                                                            ALU.mult, ALU.add))

            def beside_step(k):
                if pair_combined(k) is not None:
                    combine(pair_combined(k))
                elif k >= 3 and k % 2 and k < 9:
                    bias_part((k - 3) // 2)
                elif k % 2 and 9 <= k < 15:
                    bias_row_of((k - 9) // 2)
                i = k - 20
                if 20 <= k and k % 2 == 0 and (k - 20) // 2 < KT:
                    i = (k - 20) // 2
                    dve.wait_ge(s_pair, 2 * KT + i + 1)
                    nc.vector.tensor_reduce(m_amax[:, i:i + 1], m_sb[:, i], AX.X, ALU.max,
                                            apply_absolute_value=True).then_inc(s_mamax, 1)
                if k == 27:
                    dve.wait_ge(s_mamax, KT)
                    nc.vector.tensor_reduce(amax[:, 3:4], m_amax[:], AX.X, ALU.max).then_inc(s_amax, 1)
                if k == 28:
                    dve.wait_ge(s_amax_all, 2)
                    scales(3, 4)
                    wait_own(nc.vector.tensor_scalar(fb_ones[:], ones_sb[:], scale[:, 3:4], ROW_SCALE,
                                                     ALU.mult, ALU.mult))
                if k in (29, 30):
                    for i in ((0, 1) if k == 29 else (2, 3)):
                        split(m_hi[:, i], m_lo[:, i], m_sb[:, i], 3)
                    if k == 30:
                        nc.vector.sem_inc(s_msplit, 1)

            dve.wait_ge(s_del, QUADS)
            last_step = h_sb[:, CHUNK - 1::CHUNK]

            def scan_round(r, k0, lows0):
                if not (isinstance(r, int) and r == 0):
                    dve.wait_ge(s_h, k0)
                    nc.vector.tensor_copy(ends[:], last_step)
                    for b in range(2):
                        a, z = b * BATCH_LANES, (b + 1) * BATCH_LANES
                        last = nc.vector.tensor_tensor(
                            hd_first[:, a + 1:z], h_sb[:, a * CHUNK + CHUNK - 1:(z - 1) * CHUNK:CHUNK],
                            del_sb[:, (a + 1) * CHUNK:z * CHUNK:CHUNK], ALU.mult)
                    last.then_inc(s_hd, 1)
                for s in range(CHUNK):
                    dve.wait_ge(s_h, k0 + s + 1)
                    if s + 1 < CHUNK:
                        nc.vector.tensor_tensor(hd[:], h_sb[:, s::CHUNK], del_sb[:, s + 1::CHUNK],
                                                ALU.mult).then_inc(s_hd, 1)
                    if isinstance(r, int):
                        beside_step(k0 + s)
                    if lows0 is not None:
                        dve.wait_ge(s_low, lows0 + s + 1)
                        last = nc.vector.scalar_tensor_tensor(h16[:, s::CHUNK], h_sb[:, s::CHUNK],
                                                              STATE_SCALE, h16[:, s::CHUNK], ALU.mult,
                                                              ALU.add)
                if lows0 is not None:
                    last.then_inc(s_split, 1)

            nc.vector.sem_inc(s_hd, 1)
            scan_round(0, 0, None)
            scan_round(1, CHUNK, 0)
            nc.vector.tensor_tensor(differ[:], last_step, ends[:], ALU.not_equal).then_inc(s_dscan, 1)
            dve.wait_ge(s_dscan, 1)
            nc.vector.tensor_reduce(n_differ[:], differ[:], AX.X, ALU.add).then_inc(s_cmp, 1)
            dve.wait_ge(s_cnt, 1)
            nc.vector.tensor_copy(flag[:], bank[0][0:1, 0:1]).then_inc(s_flag, 1)
            dve.wait_ge(s_flag, 1)
            changed = dve.value_load(flag[0:1, 0:1])
            with dve.If(changed > 0):
                with dve.Fori(2, BATCH_LANES) as r:
                    scan_round(r, r * CHUNK, (r - 1) * CHUNK)
                dve.wait_ge(s_split, BATCH_LANES - 1)
            dve.wait_ge(s_split, 1)
            nc.vector.sem_inc(s_h16, 1)

            def gated(n, k, v):
                dve.wait_ge(s_y, n + 1)
                if k % 4 == 0:
                    dve.wait_ge(s_bg[k // 4], v * 16 + 16)
                nc.vector.scalar_tensor_tensor(gate_sb[:, k // 4, k % 4], ps_y[k % 2][:], unscale[:, 2:3],
                                               gate_sb[:, k // 4, k % 4], ALU.mult,
                                               ALU.mult).then_inc(s_gy, 1)

            def b_statistics(n, k):
                dve.wait_ge(s_v, n + 1)
                nc.vector.bn_stats(bn[:, k % 4], x_sb[:, k // 4, k % 4]).then_inc(s_bbn, 1)

            def b_normalise(n, k):
                dve.wait_ge(s_brstd, n + 1)
                if before(n, 4):
                    dve.wait_ge(s_bt, n - 3)
                    dve.wait_ge(s_w, n - 3)
                nc.vector.tensor_scalar(norm_sb[:, k % 4], x_sb[:, k // 4, k % 4], mv[:, k % 4, 0:1],
                                        rstd[:, k % 4:k % 4 + 1], ALU.subtract,
                                        ALU.mult).then_inc(s_bnorm, 1)

            def ffn_sum(n, k):
                dve.wait_ge(s_f, n + 1)
                if before(n, 8):
                    dve.wait_ge(s_out, n - 7)
                nc.vector.scalar_tensor_tensor(w_ring[:, k], ps_g[k % 2][:], unscale[:, 3:4],
                                               norm_sb[:, k % 4], ALU.mult, ALU.add,
                                               accum_out=wsum[:, k:k + 1]).then_inc(s_w, 1)

            def slot(n, k, v):
                if exists(n + 4):
                    b_statistics(n + 4, (k + 4) % 8)
                    dve.wait_ge(s_bbn, n + 5)
                if exists(n + 2):
                    b_normalise(n + 2, (k + 2) % 8)
                if exists(n + 4):
                    aggregate(n + 4, (k + 4) % 8, s_baggr)
                if exists(n + 1):
                    low_half(n + 1, k + 1, s_bhi, s_blo)
                if exists(n + 6):
                    gated(n + 6, (k + 6) % 8, v if k < 2 else v + 1)
                if exists(n - 1):
                    ffn_sum(n - 1, (k - 1) % 8)
            run_slots(dve, -6, TILES, slot)

        @block.tensor
        def _(pe):
            pe.wait_ge(s_brep, 1)
            for t in range(KT):
                nc.tensor.matmul(bank[0][:], beta_rep[:, t], wg_raw[:, t], start=(t == 0), stop=False)
                nc.tensor.matmul(bank[2][:, 0:1], wp_rep[:, t].rearrange("p g s -> p (g s)"),
                                 beta_sb[:, t:t + 1], start=(t == 0), stop=(t == KT - 1))
            nc.tensor.matmul(bank[0][:], ones_sb[0:1, :], bias_row[0:1, 0, :], start=False, stop=True)
            nc.tensor.matmul(bank[1][:], ones_sb[0:1, :], bias_row[0:1, 1, :], start=True,
                             stop=True).then_inc(s_bias_mm, 1)
            pe.wait_ge(s_wready, 1)

            def transpose(n, k, norm_done, hi_done, lo_done, t_done):
                pe.wait_ge(norm_done, n + 1)
                if before(n, 2):
                    pe.wait_ge(hi_done, n - 1)
                    pe.wait_ge(lo_done, n - 1)
                for t in range(KT):
                    last = nc.tensor.transpose(ps_t[k % 2][:, t * P:(t + 1) * P],
                                               norm_sb[:, k % 4, t * P:(t + 1) * P], ident)
                last.then_inc(t_done, 1)

            def product(dst, k, w_hi, w_lo, start=True):
                for t in range(KT):
                    nc.tensor.matmul(dst, hi_sb[:, k % 2, t], w_hi[:, t],
                                     start=(start and t == 0), stop=False)
                    nc.tensor.matmul(dst, hi_sb[:, k % 2, t], w_lo[:, t], start=False, stop=False)
                for t in range(KT):
                    last = nc.tensor.matmul(dst, lo_sb[:, k % 2, t], w_hi[:, t], start=False,
                                            stop=(t == KT - 1))
                return last

            def products(n, k, v):
                pe.wait_ge(s_hi, n + 1)
                pe.wait_ge(s_lo, n + 1)
                if before(n, 2):
                    pe.wait_ge(s_gsum, n - 1)
                product(ps_g[k % 2][:], k, wg_hi, wg_lo).then_inc(s_gate, 1)
                if k % 4 == 0 and before(n, 8):
                    pe.wait_ge(s_zrow, v * 2 + k // 4 - 1)
                g = k % 4
                product(ps_z[k // 4][:, g * 32:(g + 1) * 32], k, wp_hi, wp_lo).then_inc(s_proj, 1)

            def z_transpose(u):
                pe.wait_ge(s_zrow, u + 1)
                if before(u, 1):
                    pe.wait_ge(s_del, u)
                    pe.wait_ge(s_z, u)
                nc.tensor.transpose(ps_x[:, 0:P], zrow[:], ident).then_inc(s_zt, 1)

            def slot(n, k, v):
                if exists(n + 1):
                    transpose(n + 1, k + 1, s_norm, s_hi, s_lo, s_t)
                if k % 4 == 1 and exists(n - 4):
                    z_transpose(v * 2 + k // 4 - 1)
                if exists(n):
                    products(n, k, v)
            run_slots(pe, -1, TILES + 1, slot)

            pe.wait_ge(s_wb, 16 * len(SCAN_A_LOADS + WB_LOADS))
            pe.wait_ge(s_gsum, TILES)
            pe.wait_ge(s_lo, TILES)
            pe.wait_ge(s_zrow, QUADS)
            pe.wait_ge(s_z, QUADS)

            def fourier_product(j):
                q = j // 2
                if q < 2 * KT:
                    i = q // 2
                    w = ((w_re_sb, w_im_sb), (w_im_sb, w_re_sb))[q % 2][j % 2]
                else:
                    i = q - 2 * KT
                    w = (pt_sb, qt_sb)[j % 2]
                    pe.wait_ge(s_pair, 2 * KT)
                if q >= 2:
                    pe.wait_ge(s_pair, q - 1)
                f = (cos_sb, sin_sb)[j % 2]
                for t in range(KT):
                    last = nc.tensor.matmul(bank[2 + 2 * (q % 2) + j % 2][:, 0:HALF],
                                            w[:, t, i * P:(i + 1) * P], f[:, t],
                                            start=(t == 0), stop=(t == KT - 1))
                last.then_inc(s_mm, 1)

            def scan_round(r, k0):
                def inputs(s):
                    nc.tensor.matmul(bank[s % 2][:, 0:LANES], select, z_sb[:, s::CHUNK],
                                     start=True, stop=False)
                if not (isinstance(r, int) and r == 0):
                    pe.wait_ge(s_h, k0)
                inputs(0)
                for s in range(CHUNK):
                    pe.wait_ge(s_hd, k0 + s + 1)
                    nc.tensor.matmul(bank[s % 2][:, 0:LANES], scan_a[:], (hd if s else hd_first)[:],
                                     start=False, stop=True).then_inc(s_pre, 1)
                    if s + 1 < CHUNK:
                        inputs(s + 1)
                    if isinstance(r, int) and on_scan_step(k0 + s) is not None:
                        fourier_product(on_scan_step(k0 + s))
            scan_round(0, 0)
            scan_round(1, CHUNK)
            pe.wait_ge(s_cmp, 1)
            nc.tensor.matmul(bank[0][0:1, 0:1], n_differ[:], ones_sb[:, 0:1], start=True,
                             stop=True).then_inc(s_cnt, 1)
            pe.wait_ge(s_flag, 1)
            changed = pe.value_load(flag[0:1, 0:1])
            with pe.If(changed > 0):
                with pe.Fori(2, BATCH_LANES) as r:
                    scan_round(r, r * CHUNK)

            pe.wait_ge(s_msplit, 1)

            def states_out(n, k, v):
                if isinstance(n, int) and n == 0:
                    pe.wait_ge(s_hrep, 4 * 16)
                if isinstance(n, int) and n == H_PIECES[0][1] // P * GROUPS:
                    pe.wait_ge(s_hrep, 8 * 16)
                if before(n, 2):
                    pe.wait_ge(s_gy, n - 1)
                u, g = v * 2 + k // 4, k % 4
                nc.tensor.matmul(ps_y[k % 2][:], h_rep[g // 2][:, bass.ts(u, P)], c_parts[:, g % 2],
                                 start=True, stop=True).then_inc(s_y, 1)

            def ffn(n, k):
                pe.wait_ge(s_bhi, n + 1)
                pe.wait_ge(s_blo, n + 1)
                if before(n, 2):
                    pe.wait_ge(s_w, n - 1)
                nc.tensor.matmul(ps_g[k % 2][:], fb_ones[:], fb_rows[:], start=True, stop=False)
                product(ps_g[k % 2][:], k, m_hi, m_lo, start=False).then_inc(s_f, 1)

            def slot(n, k, v):
                if exists(n + 1):
                    transpose(n + 1, k + 1, s_bnorm, s_bhi, s_blo, s_bt)
                if exists(n + 7):
                    states_out(n + 7, (k + 7) % 8, v if k < 1 else v + 1)
                if exists(n):
                    ffn(n, k)
            run_slots(pe, -7, TILES - 1, slot)


_INS = ["L0_attn_x", "L0_attn_ln_gamma", "L0_attn_ln_beta", "L0_attn_A", "L0_attn_C", "L0_attn_w_delta",
        "L0_attn_b_delta", "L0_attn_w_in", "L0_attn_b_in", "L0_attn_w_gate", "L0_attn_b_gate",
        "L0_ffn_w_freq_real", "L0_ffn_w_freq_imag", "L0_ffn_bias"]


def shape_constants():
    c = np.zeros((P, C_WIDTH), np.float32)
    c[:, C_IDENT:C_IDENT + P] = np.eye(P)
    for g in range(GROUPS):
        for s in range(STATE):
            k = g * 32 + STATE + s
            c[k, C_SELECT + g * 32 + s] = c[k, C_SELECT + g * 32 + STATE + s] = 1.0
            c[k, C_LOW_STATE] = -STATE_SCALE
        c[g * 32:(g + 1) * 32, C_GROUP + g % 2] = 1.0
    c[P // 2:, C_LOW_C] = -1.0
    for i in range(3):
        c[i, C_PART + i] = 1.0
    return c


def fourier_constants():
    jk = np.outer(np.arange(D), np.arange(HALF)) % D
    a = 2.0 * np.pi * jk / D
    return np.stack([np.cos(a), np.sin(a)]).astype(np.float32)


def kernel(**inputs):
    import concourse.bacc as _bacc
    from concourse.bass_utils import run_bass_kernel_spmd as _run

    nc = _bacc.Bacc("TRN2", target_bir_lowering=False, num_devices=1)
    arrays = {name: np.ascontiguousarray(inputs[name]) for name in _INS}
    arrays["L0_attn_x"] = arrays["L0_attn_x"].reshape(BATCH * SEQ, D)
    for name in ("L0_attn_ln_gamma", "L0_attn_ln_beta"):
        arrays[name] = np.ascontiguousarray(arrays[name].reshape(KT, P).T)
    arrays["shape_constants"] = shape_constants()
    arrays["fourier_constants"] = fourier_constants()
    args = [nc.dram_tensor(k, a.shape, mybir.dt.from_np(a.dtype), kind="ExternalInput").ap()
            for k, a in arrays.items()]
    out = nc.dram_tensor("out", (BATCH * SEQ, D), F32, kind="ExternalOutput").ap()
    gate_dram = nc.dram_tensor("gate_dram", (BATCH * SEQ, D), F32, kind="Internal").ap()
    build(nc, *args, out, gate_dram)
    r = _run(nc, [arrays], core_ids=[0])
    return r.results[0]["out"].reshape(BATCH, SEQ, D)
```

```python
from contextlib import ExitStack

import numpy as np

import concourse.bass as bass
from concourse import mybir

P = 128
BATCH, SEQ, D = 8, 2048, 512
STATE = 16
KT = D // P
OCTETS = SEQ // P
TILES = OCTETS * BATCH
HALF = D // 2 + 1
CHUNK = 16
LANES = SEQ // CHUNK
STEPS = 2 * CHUNK
PAIRS = 3 * KT
LN_EPS = 1e-5
SPLIT_TOP = 2.0 ** 14
ROW_SCALE = 2.0 ** 11
STATE_SCALE = 2.0 ** 14
WAVE_SCALE = 2.0 ** 14
LIFT = 1.0 / 8

ALU = mybir.AluOpType
ACT = mybir.ActivationFunctionType
F32 = mybir.dt.float32
F16 = mybir.dt.float16
I32 = mybir.dt.int32
AX = mybir.AxisListType
ABSMAX = bass.bass_isa.ReduceOp.absmax
SUM = bass.bass_isa.ReduceOp.add

C_IDENT, C_BLOCKS = 0, P
C_PARTS = 2 * P
C_WIDTH = C_PARTS + 4
W_GAMMA, W_BETA, W_BIAS = 0, KT, 2 * KT
W_PROJ = W_BIAS + 2
W_ROW0 = W_PROJ + KT * 2 * STATE
W_WIDTH = W_ROW0 + 2 * KT


def exists(n):
    return not isinstance(n, int) or 0 <= n < TILES


def before(n, k):
    return not isinstance(n, int) or n >= k


def run_slots(engine, first, last, slot):
    for n in range(first, 8):
        slot(n, n % 8, n // 8)
    with engine.Fori(1, OCTETS - 1) as v:
        for k in range(8):
            slot(v * 8 + k, k, v)
    for n in range(TILES - 8, last + 1):
        slot(n, n % 8, n // 8)


def build(nc, x, small, a_and_c, bias_rows, w_gate, w_re, w_im, consts, dft, dft_halves,
          out, gate_dram):
    ctx = ExitStack()
    with ctx:
        def sb(name, shape, dt=F32):
            return ctx.enter_context(nc.sbuf_tensor(name, shape, dt))

        def sem(name):
            return ctx.enter_context(nc.semaphore(name))

        x_sb = sb("x_sb", [P, 2, 4, D])
        gate_sb = sb("gate_sb", [P, 2, 4, D])
        out_sb = sb("out_sb", [P, 2, 4, D])
        norm_sb = sb("norm_sb", [P, 4, D])
        hi_sb = sb("hi_sb", [P, 2, KT, P], F16)
        lo_sb = sb("lo_sb", [P, 2, KT, P], F16)
        gsum_sb = sb("gsum_sb", [P, 2, D])
        w_ring = sb("w_ring", [P, 2 * KT, D])
        wg_raw = w_ring[:, 0:KT]
        c_first = w_ring[:].rearrange("p t d -> p (t d)").bitcast(F16).rearrange(
            "p (b h d) -> p b h d", b=BATCH, h=2)
        wg_hi = sb("wg_hi", [P, KT, D], F16)
        wg_lo = sb("wg_lo", [P, KT, D], F16)
        small_sb = sb("small_sb", [P, W_WIDTH])
        gamma_sb, beta_sb = small_sb[:, W_GAMMA:W_GAMMA + KT], small_sb[:, W_BETA:W_BETA + KT]
        wp_raw = small_sb[:, W_PROJ:W_ROW0].rearrange("p (t n) -> p t n", t=KT)
        a_c_sb = sb("a_c_sb", [P, P + D])
        a_rep, c_rep = a_c_sb[:, 0:P], a_c_sb[:, P:P + D]
        wp_rep = sb("wp_rep", [P, 2, KT, BATCH, STATE])
        wp_fold = sb("wp_fold", [P, KT, 2 * STATE])
        wp_halves = sb("wp_halves", [P, KT, 2, 2 * STATE], F16)
        beta_rep = sb("beta_rep", [P, KT, P])
        bias_row = sb("bias_row", [1, 2, D])
        ones_sb = sb("ones_sb", [P, P])
        gbias_sb = sb("gbias_sb", [P, D])
        fbias_sb = sb("fbias_sb", [P, D])
        fbias_even, fbias_odd = sb("fbias_even", [P, HALF]), sb("fbias_odd", [P, HALF])
        shift = sb("shift", [P, 2, KT])
        bias_max = sb("bias_max", [P, 1])
        w_abs = sb("w_abs", [P, 4])
        w_abs_sum = sb("w_abs_sum", [P, 1])
        w_abs_all = sb("w_abs_all", [P, 1])
        warm = sb("warm", [P, 1])
        zbias = sb("zbias", [P, 2])
        cst = sb("cst", [P, C_WIDTH])
        ident = cst[:, C_IDENT:C_IDENT + P]
        scan_a = sb("scan_a", [P, P])
        c_hi, c_lo = sb("c_hi", [P, D], F16), sb("c_lo", [P, D], F16)
        c_parts = sb("c_parts", [P, 2, D], F16)
        row_max = sb("row_max", [P, KT])
        row_max_g = sb("row_max_g", [P, KT])
        g_scale = sb("g_scale", [P, KT])
        amax = sb("amax", [P, 3])
        amax_all = sb("amax_all", [P, 4])
        amax_pos = sb("amax_pos", [P, 4])
        pow2 = sb("pow2", [P, 4])
        pow2_inv = sb("pow2_inv", [P, 4])
        scale = sb("scale", [P, 4])
        unscale = sb("unscale", [P, 4])
        z_low = sb("z_low", [P, 2, 4, 2 * STATE])
        zrow = sb("zrow", [P, 2, BATCH, STATE])
        z_sb = sb("z_sb", [P, SEQ])
        del_sb = sb("del_sb", [P, SEQ])
        h_sb = sb("h_sb", [P, SEQ])
        h_hi = sb("h_hi", [P, SEQ], F16)
        h_lo = sb("h_lo", [P, SEQ], F16)
        h_rep = sb("h_rep", [P, BATCH // 2, SEQ], F16)
        hd = sb("hd", [P, LANES])
        hd_first = sb("hd_first", [P, LANES])
        ends = sb("ends", [P, LANES])
        differ = sb("differ", [P, LANES])
        n_differ = sb("n_differ", [P, 1])
        flag = sb("flag", [1, 1], I32)
        w_re_sb = sb("w_re_sb", [P, KT, D])
        w_im_sb = sb("w_im_sb", [P, KT, D])
        cos_halves = sb("cos_halves", [P, KT, 2, HALF], F16)
        sin_halves = sb("sin_halves", [P, KT, 2, HALF], F16)
        wave_sb = h_rep[:].bitcast(F32)
        cos_sb, sin_sb = wave_sb[:, :, 0:HALF], wave_sb[:, :, D:D + HALF]
        even_sb = sb("even_sb", [P, 2, HALF])
        def halves_in(tile):
            h = tile.bitcast(F16)
            return h[:, :, 0:D], h[:, :, D:2 * D]

        w_re_halves, w_im_halves = halves_in(out_sb[:, 0]), halves_in(out_sb[:, 1])
        pt_halves, qt_halves = halves_in(w_re_sb[:]), halves_in(w_im_sb[:])
        pq_sb = gsum_sb
        m_sb = out_sb[:, 0]
        m_hi, m_lo = halves_in(z_sb[:].rearrange("p (t n) -> p t n", t=KT))
        w_max, w_max_all = sb("w_max", [P, 1]), sb("w_max_all", [P, 1])
        w_pow2 = sb("w_pow2", [P, 1])
        w_scale = sb("w_scale", [P, 1])
        p_scale = sb("p_scale", [P, 1])
        p_ratio = sb("p_ratio", [P, 2])
        bn = sb("bn", [P, 4, 6])
        mv = sb("mv", [P, 4, 2])
        veps = sb("veps", [P, 4])
        rstd = sb("rstd", [P, 4])
        scaled_mean = sb("scaled_mean", [P, 4])
        lift_bias = sb("lift_bias", [P, 4])
        c_lift = sb("c_lift", [P, 1])
        c_eps = sb("c_eps", [P, 1])
        c_eps4 = sb("c_eps4", [P, 1])
        c_half = sb("c_half", [P, 2])
        wsum = sb("wsum", [P, 8])
        negmu = sb("negmu", [P, 8])
        vsum = sb("vsum", [P, 8])
        var2 = sb("var2", [P, 8])
        rnorm2 = sb("rnorm2", [P, 8])
        rstd2 = sb("rstd2", [P, 8])
        c_mean = sb("c_mean", [P, 1])
        c_epsd = sb("c_epsd", [P, 2])
        c_rootd = sb("c_rootd", [P, 2])
        nbias2 = sb("nbias2", [P, 8])

        bank = [ctx.enter_context(nc.psum_tensor(f"bank{i}", [P, 512], F32)) for i in range(8)]
        ps_t, ps_g, ps_z, ps_x, ps_y = bank[0:2], bank[2:4], bank[4:6], bank[6], bank[6:8]

        def c_share(i):
            column = C_BLOCKS + i // 2 * STATE
            return i // 2, i % 2, cst[:, column:column + 1]

        def tiles_of(t):
            return t.rearrange("(q b v p) d -> v q p b d", q=2, b=4, p=P)

        def z_parts(q):
            return ps_z[q][:, 0:8 * 2 * STATE].rearrange("p (b h n) -> p b h n", b=4, h=2)

        x_v, out_v, gate_v = tiles_of(x), tiles_of(out), tiles_of(gate_dram)

        s_small = sem("small_weights_loaded")
        s_cst = sem("constants_loaded")
        s_a_c = sem("a_and_c_loaded")
        s_wg = [sem(f"gate_weights_loaded{i}") for i in range(2)]
        s_xfirst = sem("first_tiles_loaded")
        s_brow = sem("bias_rows_loaded")
        s_zbias = sem("biases_ready")
        s_scale = sem("scales_ready")
        s_wg_hi = sem("gate_weights_high")
        s_m_hi = sem("m_high")
        s_mscale = sem("m_scale_ready")
        s_zlow = sem("a_zlow")
        s_final = sem("scan_general_done")
        s_hrep2 = [sem(f"h_rep_loaded_again{r}") for r in range(BATCH // 2)]
        s_wb = sem("fourier_loaded")
        s_folded = sem("ffn_bias_folded")
        s_c_split = sem("c_split")
        s_c_first = sem("c_for_first_octet")
        s_w_abs = sem("fourier_weights_summed")
        s_w_abs_sum = sem("fourier_weights_sum")
        s_w_abs_all = sem("fourier_weights_sum_reduced")
        s_w_scale = sem("fourier_weights_scale")
        s_w_hi = sem("fourier_weights_high")
        s_w_lo = sem("fourier_weights_low")
        s_pfull = sem("pq_combined")
        s_p_hi = sem("pq_high")
        s_bmr = sem("b_scaled_mean")
        s_blift = sem("b_lift_bias")
        s_pool_const = sem("small_constants_written")
        s_dve = sem("dve_step")
        s_amax = sem("amax_ready")
        s_amax_all = sem("amax_reduced")
        s_ones = sem("ones_ready")
        s_brep = sem("beta_replicated")
        s_wprep = sem("projection_weights_replicated")
        s_bias_mm = sem("bias_products")
        s_wready = sem("weights_split")
        s_xl = [sem(f"x_loaded{i}") for i in range(2)]
        s_gst = [sem(f"gate_stored{i}") for i in range(2)]
        s_bn = sem("a_bn")
        s_aggr = sem("a_variance")
        s_veps = sem("a_variance_eps")
        s_rstd = sem("a_rstd")
        s_norm = sem("a_norm")
        s_t = sem("a_transposed")
        s_hi = sem("a_hi")
        s_lo = sem("a_lo")
        s_gate = sem("a_gate_products")
        s_proj = sem("a_projections")
        s_gsum = sem("a_gate_logits")
        s_gsig = sem("a_gate")
        s_zrow = sem("a_zrow")
        s_zt = sem("a_z_transposed")
        s_del = sem("a_delta")
        s_z = sem("a_z")
        s_mm = sem("m_products")
        s_even = sem("m_even_copied")
        s_pair = sem("m_pair_combined")
        s_msplit = sem("m_split")
        s_high = sem("scan_high_half")
        s_hrep = [sem(f"h_rep_loaded{r}") for r in range(BATCH // 2)]
        s_hd = sem("scan_hd")
        s_pre = sem("scan_pre")
        s_h = sem("scan_h")
        s_cmp = sem("scan_compared")
        s_cnt = sem("scan_counted")
        s_flag = sem("scan_flag")
        s_seen = sem("scan_flag_seen")
        s_round_act = sem("scan_rounds_of_scalar")
        s_round_dve = sem("scan_rounds_of_vector")
        s_last = sem("b_last_stored")
        s_dscan = sem("scan_dve")
        s_split = sem("scan_split")
        s_bx = [sem(f"b_x_loaded{i}") for i in range(2)]
        s_bg = [sem(f"b_gate_loaded{i}") for i in range(2)]
        s_bst = [sem(f"b_stored{i}") for i in range(2)]
        s_y = sem("b_y")
        s_gy = sem("b_gated")
        s_v = sem("b_v")
        s_bbn = sem("b_bn")
        s_baggr = sem("b_variance")
        s_bveps = sem("b_variance_eps")
        s_brstd = sem("b_rstd")
        s_bnorm = sem("b_norm")
        s_bt = sem("b_transposed")
        s_bhi = sem("b_hi")
        s_blo = sem("b_lo")
        s_f = sem("b_ffn_products")
        s_w = sem("b_w")
        s_negmu = sem("b_negmu")
        s_sq = sem("b_squares")
        s_var2 = sem("b_var2")
        s_rnorm2 = sem("b_rnorm2")
        s_rstd2 = sem("b_rstd2")
        s_nb2 = sem("b_nbias2")
        s_out = sem("b_out")
        s_out_last = sem("b_out_last")

        PRODUCT = 3 * KT
        matmuls_until = [2 * PRODUCT + (27 * (s + 1) + 3) // 4 for s in range(STEPS)]
        LATE = matmuls_until[-1] // PRODUCT

        ORDER = list(range(4 * KT)) + [4 * KT, 4 * KT + 2, 4 * KT + 1, 4 * KT + 3]
        ORDER += range(len(ORDER), 2 * PAIRS)

        def products_with(j):
            return ORDER.index(j) + 1

        def step_after(j):
            return next(s for s in range(STEPS) if matmuls_until[s] >= PRODUCT * products_with(j)) + 1

        copies_beside = {step_after(2 * q): q for q in range(LATE // 2)}
        combined_beside = {step_after(2 * q + 1): q for q in range(LATE // 2)}

        block = ctx.enter_context(nc.Block())

        @block.sync
        def _(sp):
            def load_x(v, q, loaded):
                sp.dma_start(x_sb[:, q], x_v[v, q]).then_inc(loaded[q], 16)

            def first_pass(v, q):
                if not isinstance(v, int):
                    sp.wait_ge(s_norm, v * 8 + 4 * q + 4)
                    load_x(v + 1, q, s_xl)
                sp.wait_ge(s_gsig, v * 8 + 4 * q + 4)
                sp.dma_start(gate_v[v, q], gate_sb[:, q]).then_inc(s_gst[q], 16)

            sp.dma_start(x_sb[:, 0, 0:2], x_v[0, 0][:, 0:2]).then_inc(s_xfirst, 16)
            for i in range(2):
                t = slice(i * KT // 2, (i + 1) * KT // 2)
                sp.dma_start(wg_raw[:, t], w_gate.rearrange("(t p) n -> p t n", p=P)[:, t]).then_inc(s_wg[i], 16)
            sp.dma_start(x_sb[:, 0, 2:4], x_v[0, 0][:, 2:4]).then_inc(s_xl[0], 16)
            load_x(0, 1, s_xl)
            with sp.Fori(0, OCTETS - 1) as v:
                first_pass(v, 0)
                first_pass(v, 1)
            first_pass(OCTETS - 1, 0)
            first_pass(OCTETS - 1, 1)

            def load_gate(v, q):
                sp.dma_start(gate_sb[:, q], gate_v[v, q]).then_inc(s_bg[q], 16)

            def store_result(v, q):
                sp.wait_ge(s_out, v * 8 + 4 * q + 4)
                sp.dma_start(out_v[v, q], out_sb[:, q]).then_inc(s_bst[q], 16)

            def second_pass(v, q):
                sp.wait_ge(s_v, v * 8 + 4 * q + 4)
                load_gate(v + 1, q)
                if not isinstance(v, int):
                    store_result(v - 1, q)
                sp.wait_ge(s_bnorm, v * 8 + 4 * q + 4)
                load_x(v + 1, q, s_bx)

            def replicate_states(done):
                for r in range(BATCH // 2):
                    for seg in range(4):
                        src = (h_hi, h_hi, h_lo, h_lo)[seg]
                        sp.dma_start(h_rep[32 * seg:32 * seg + 32, r, P:SEQ],
                                     src[32 * r:32 * r + 32, P:SEQ]).then_inc(done[r], 16)

            sp.wait_ge(s_norm, TILES)
            for q in range(2):
                sp.wait_ge(s_gst[q], 16 * OCTETS)
            for q in range(2):
                load_x(0, q, s_bx)
                load_gate(0, q)
            sp.wait_ge(s_split, 1)
            replicate_states(s_hrep)
            sp.wait_ge(s_flag, 1)
            changed = sp.value_load(flag[0:1, 0:1])
            sp.sem_inc(s_seen, 1)
            with sp.If(changed > 0):
                for r in range(BATCH // 2):
                    sp.wait_ge(s_hrep[r], 4 * 16)
                sp.wait_ge(s_final, 1)
                replicate_states(s_hrep2)
            second_pass(0, 0)
            second_pass(0, 1)
            with sp.Fori(1, OCTETS - 1) as v:
                second_pass(v, 0)
                second_pass(v, 1)
            for v in (OCTETS - 2, OCTETS - 1):
                for q in range(2):
                    if v < OCTETS - 1 or q == 0:
                        store_result(v, q)
            for b in range(4):
                if b < 3:
                    sp.wait_ge(s_out, TILES - 3 + b)
                else:
                    sp.wait_ge(s_out_last, 1)
                sp.dma_start(out_v[OCTETS - 1, 1][:, b], out_sb[:, 1, b]).then_inc(s_last, 16)
            sp.wait_ge(s_bst[0], 16 * OCTETS)
            sp.wait_ge(s_bst[1], 16 * (OCTETS - 1))
            sp.wait_ge(s_last, 16 * 4)

        WB_LOADS = [
            (w_re_sb[:], w_re.rearrange("(t p) n -> p t n", p=P)),
            (w_im_sb[:], w_im.rearrange("(t p) n -> p t n", p=P)),
            (cos_sb, dft[0].rearrange("(t p) n -> p t n", p=P)),
            (sin_sb, dft[1].rearrange("(t p) n -> p t n", p=P)),
            (cos_halves[:], dft_halves[0].rearrange("(t p) h n -> p t h n", p=P)),
            (sin_halves[:], dft_halves[1].rearrange("(t p) h n -> p t h n", p=P)),
        ]

        @block.scalar
        def _(act):
            act.dma_start(small_sb[:], small).then_inc(s_small, 16)
            act.dma_start(cst[:], consts).then_inc(s_cst, 16)
            act.wait_ge(s_pool_const, 1)
            nc.scalar.activation(warm[:], c_eps[:], ACT.Sigmoid)
            act.dma_start(bias_row[:], bias_rows).then_inc(s_brow, 16)
            act.wait_ge(s_small, 16)
            act.wait_ge(s_ones, 1)
            for t in range(KT):
                last = nc.scalar.activation(beta_rep[:, t], ones_sb[:], ACT.Copy, scale=beta_sb[:, t:t + 1])
            last.then_inc(s_brep, 1)
            act.dma_start(a_c_sb[:], a_and_c).then_inc(s_a_c, 16)
            for dst, src in WB_LOADS:
                act.dma_start(dst, src).then_inc(s_wb, 16)

            def hi(n, k):
                act.wait_ge(s_t, n + 1)
                if before(n, 2):
                    act.wait_ge(s_proj, n - 1)
                nc.scalar.activation(hi_sb[:, k % 2], ps_t[k % 2][:], ACT.Copy,
                                     scale=ROW_SCALE).then_inc(s_hi, 1)

            def sigmoid_gate(n, k, v):
                act.wait_ge(s_gsum, n + 1)
                if k % 4 == 0 and before(n, 8):
                    act.wait_ge(s_gst[k // 4], v * 16)
                nc.scalar.activation(gate_sb[:, k // 4, k % 4], gsum_sb[:, k % 2],
                                     ACT.Sigmoid).then_inc(s_gsig, 1)

            def copy_z_low(v, q):
                act.wait_ge(s_proj, v * 8 + 4 * q + 4)
                if before(v, 1):
                    act.wait_ge(s_zrow, v * 2 + q - 1)
                nc.scalar.activation(z_low[:, q], z_parts(q)[:, :, 1], ACT.Copy).then_inc(s_zlow, 1)

            def delta(v):
                act.wait_ge(s_zt, v + 1)
                if isinstance(v, int) and v == 0:
                    act.wait_ge(s_zbias, 1)
                nc.scalar.activation(del_sb[:, bass.ts(v, P)], ps_x[:, 0:P], ACT.Sigmoid,
                                     bias=zbias[:, 0:1], scale=unscale[:, 1:2]).then_inc(s_del, 1)

            def gate_weights_high():
                act.wait_ge(s_scale, 1)
                for t in range(KT):
                    nc.scalar.activation(wg_hi[:, t], wg_raw[:, t], ACT.Copy,
                                         scale=g_scale[:, t:t + 1]).then_inc(s_wg_hi, 1)

            def c_for_batch(i):
                b, h, mask = c_share(i)
                act.wait_ge(s_cst, 16)
                act.wait_ge(s_c_split, 1)
                nc.scalar.activation(c_first[:, b, h], (c_hi, c_lo)[h][:], ACT.Copy,
                                     scale=mask).then_inc(s_c_first, 1)

            def sum_weights(i):
                act.wait_ge(s_wb, 16 * len(WB_LOADS))
                w = (w_re_sb, w_im_sb)[i // 2][:, 2 * (i % 2):2 * (i % 2) + 2]
                nc.scalar.activation(h_sb[:, 0:2 * D] if i % 2 else h_sb[:, 2 * D:4 * D],
                                     w.rearrange("p t n -> p (t n)"), ACT.Abs,
                                     accum_out=w_abs[:, i:i + 1]).then_inc(s_w_abs, 1)

            def frequency_weights_high(i):
                act.wait_ge(s_w_scale, 1)
                w, halves = ((w_re_sb, w_re_halves), (w_im_sb, w_im_halves))[i // KT]
                nc.scalar.activation(halves[0][:, i % KT], w[:, i % KT], ACT.Copy,
                                     scale=w_scale[:, 0:1]).then_inc(s_w_hi, 1)

            def slot(n, k, v):
                if exists(n + 1):
                    hi(n + 1, k + 1)
                if isinstance(n, int) and n == -1:
                    gate_weights_high()
                if k % 4 == 0 and exists(n - 4):
                    copy_z_low(v if k else v - 1, 0 if k else 1)
                if exists(n - 2):
                    sigmoid_gate(n - 2, (k - 2) % 8, v if k >= 2 else v - 1)
                if k == 3 and exists(n - 8):
                    delta(v - 1)
                if isinstance(n, int) and 4 <= n < 8:
                    sum_weights(n - 4)
                    c_for_batch(n + 6)
                if isinstance(n, int) and n in (TILES - 8, TILES - 7):
                    c_for_batch(n - TILES + 22)
                if isinstance(n, int) and TILES - 7 < n < TILES - 2:
                    frequency_weights_high(2 * (n - TILES + 6))
                    frequency_weights_high(2 * (n - TILES + 6) + 1)
            run_slots(act, -1, TILES + 3, slot)

            def copy_even(q):
                act.wait_ge(s_mm, products_with(2 * q))
                if q == 0:
                    act.wait_ge(s_mscale, 1)
                if q >= 2:
                    act.wait_ge(s_pfull if q - 2 < 2 * KT else s_pair, q - 1)
                even, src = even_sb[:, q % 2], bank[2 + 2 * (q % 2)][:, 0:HALF]
                if q < 2 * KT:
                    nc.scalar.activation(even, src, ACT.Identity, bias=shift[:, q % 2, q // 2:q // 2 + 1],
                                         scale=p_ratio[:, 0:1]).then_inc(s_even, 1)
                else:
                    nc.scalar.activation(even, src, ACT.Copy, scale=1.0 / WAVE_SCALE).then_inc(s_even, 1)

            def high_pq(q):
                act.wait_ge(s_pfull, q + 1)
                nc.scalar.activation((pt_halves, qt_halves)[q % 2][0][:, q // 2], pq_sb[:, q % 2],
                                     ACT.Copy).then_inc(s_p_hi, 1)

            def scan_round(k0, his0):
                for s in range(CHUNK):
                    act.wait_ge(s_pre, k0 + s + 1)
                    nc.scalar.activation(h_sb[:, s::CHUNK], bank[s % 2][:, 0:LANES],
                                         ACT.Tanh).then_inc(s_h, 1)
                    if isinstance(k0, int) and k0 + s in copies_beside:
                        copy_even(copies_beside[k0 + s])
                    if isinstance(k0, int) and combined_beside.get(k0 + s - 1, 2 * KT) < 2 * KT:
                        high_pq(combined_beside[k0 + s - 1])
                    if his0 is not None:
                        act.wait_ge(s_h, k0 + s + 1)
                        nc.scalar.activation(h_hi[:, s::CHUNK], h_sb[:, s::CHUNK], ACT.Copy,
                                             scale=STATE_SCALE).then_inc(s_high, 1)
            scan_round(0, None)
            scan_round(CHUNK, 0)
            act.wait_ge(s_flag, 1)
            changed = act.value_load(flag[0:1, 0:1])
            with act.If(changed > 0):
                for r in range(BATCH // 2):
                    act.wait_ge(s_hrep[r], 4 * 16)
                with act.Fori(2, LANES) as r:
                    again = act.value_load(flag[0:1, 0:1])
                    with act.If(again > 0):
                        scan_round(r * CHUNK, (r - 1) * CHUNK)
                        act.wait_ge(s_flag, r)
                        act.sem_inc(s_round_act, 1)

            def high_m(i):
                act.wait_ge(s_pair, 2 * KT + i + 1)
                nc.scalar.activation(m_hi[:, i], m_sb[:, i], ACT.Copy).then_inc(s_m_hi, 1)

            for i in range(KT):
                if (2 * KT + i) * 2 >= LATE:
                    copy_even(2 * KT + i)
                if i:
                    high_m(i - 1)
            high_m(KT - 1)

            def b_hi(n, k):
                act.wait_ge(s_bt, n + 1)
                if before(n, 2):
                    act.wait_ge(s_f, n - 1)
                nc.scalar.activation(hi_sb[:, k % 2], ps_t[k % 2][:], ACT.Copy,
                                     scale=ROW_SCALE).then_inc(s_bhi, 1)

            def b_normalise(n, k):
                act.wait_ge(s_blift, n + 1)
                if before(n, 4):
                    act.wait_ge(s_bt, n - 3)
                    act.wait_ge(s_w, n - 3)
                nc.scalar.activation(norm_sb[:, k % 4], x_sb[:, k // 4, k % 4], ACT.Identity,
                                     bias=lift_bias[:, k % 4:k % 4 + 1],
                                     scale=rstd[:, k % 4:k % 4 + 1]).then_inc(s_bnorm, 1)

            def squares(n, k):
                act.wait_ge(s_negmu, n + 1)
                if before(n, 2):
                    act.wait_ge(s_sq, n - 1)
                nc.scalar.activation(gsum_sb[:, k % 2], w_ring[:, k], ACT.Square, bias=negmu[:, k:k + 1],
                                     accum_out=vsum[:, k:k + 1]).then_inc(s_sq, 1)

            def result(n, k, v):
                act.wait_ge(s_nb2, v * 4 + k // 2 + 1)
                if k % 4 == 0 and before(n, 8):
                    act.wait_ge(s_bst[k // 4], v * 16)
                nc.scalar.activation(out_sb[:, k // 4, k % 4], w_ring[:, k], ACT.Identity,
                                     bias=nbias2[:, k:k + 1], scale=rstd2[:, k:k + 1]).then_inc(s_out, 1)

            def slot(n, k, v):
                if exists(n + 1):
                    b_hi(n + 1, k + 1)
                if exists(n + 2):
                    b_normalise(n + 2, (k + 2) % 8)
                if exists(n - 5) and not (isinstance(n, int) and n - 5 == TILES - 1):
                    result(n - 5, (k - 5) % 8, v if k >= 5 else v - 1)
                if exists(n - 2):
                    squares(n - 2, (k - 2) % 8)
            run_slots(act, -2, TILES + 4, slot)

        @block.gpsimd
        def _(pool):
            pool.memset(c_eps[:], LN_EPS)
            pool.memset(c_eps4[:], LN_EPS / 4)
            pool.memset(c_mean[:], -1.0 / D)
            pool.memset(c_lift[:], LIFT)
            pool.memset(c_epsd[:], LN_EPS * D)
            pool.memset(c_rootd[:], float(np.sqrt(D)))
            pool.memset(c_half[:], -0.5).then_inc(s_pool_const, 1)
            pool.wait_ge(s_pool_const, 1)

            def rstd_of(n, k, var_ready, veps_ready, rstd_ready, eps):
                c = slice(k % 4, k % 4 + 1)
                pool.wait_ge(var_ready, n + 1)
                pool.tensor_tensor(veps[:, c], mv[:, k % 4, 1:2], eps[:], ALU.add).then_inc(veps_ready, 1)
                pool.wait_ge(veps_ready, n + 1)
                pool.tensor_tensor(rstd[:, c], veps[:, c], c_half[:, 0:1], ALU.pow).then_inc(rstd_ready, 1)

            def fold_bias():
                mirror = fbias_sb[:, D - 1:HALF - 1:-1]
                pool.wait_ge(s_zbias, 1)
                for edge in (0, HALF - 1):
                    pool.tensor_copy(fbias_even[:, edge:edge + 1], fbias_sb[:, edge:edge + 1])
                pool.tensor_tensor(fbias_even[:, 1:HALF - 1], fbias_sb[:, 1:HALF - 1], mirror,
                                   ALU.add).then_inc(s_folded, 1)
                pool.tensor_tensor(fbias_odd[:, 1:HALF - 1], mirror, fbias_sb[:, 1:HALF - 1],
                                   ALU.subtract).then_inc(s_folded, 1)

            def c_for_batch(i):
                b, h, mask = c_share(i)
                pool.wait_ge(s_cst, 16)
                pool.wait_ge(s_c_split, 1)
                pool.tensor_scalar(c_first[:, b, h], (c_hi, c_lo)[h][:], mask, None,
                                   ALU.mult).then_inc(s_c_first, 1)

            def slot(n, k, v):
                if exists(n + 3):
                    rstd_of(n + 3, (k + 3) % 8, s_aggr, s_veps, s_rstd, c_eps)
                if isinstance(n, int) and n == -2:
                    pool.wait_ge(s_amax, 1)
                    pool.partition_all_reduce(amax_all[:, 0:2], amax[:, 0:2], P,
                                              ABSMAX).then_inc(s_amax_all, 1)
                if isinstance(n, int) and n == 2:
                    pool.wait_ge(s_amax, 2)
                    pool.partition_all_reduce(amax_all[:, 2:3], amax[:, 2:3], P,
                                              ABSMAX).then_inc(s_amax_all, 1)
                if isinstance(n, int) and n == TILES - 8:
                    pool.wait_ge(s_w_abs_sum, 1)
                    pool.partition_all_reduce(w_abs_all[:], w_abs_sum[:], P, SUM).then_inc(s_w_abs_all, 1)
                    pool.partition_all_reduce(w_max_all[:], w_max[:], P, ABSMAX).then_inc(s_w_abs_all, 1)
                if isinstance(n, int) and n == 3:
                    fold_bias()
                if isinstance(n, int) and 4 <= n < 8:
                    c_for_batch(n - 4)
                if isinstance(n, int) and TILES - 8 <= n < TILES - 2:
                    c_for_batch(n - TILES + 12)
            run_slots(pool, -3, TILES - 1, slot)

            for q in range(2 * KT):
                high, low = (h[:, q // 2] for h in (pt_halves, qt_halves)[q % 2])
                pool.wait_ge(s_p_hi, q + 1)
                pool.tensor_tensor(low, pq_sb[:, q % 2], high, ALU.subtract).then_inc(s_pair, 1)

            def residual(n, k, v):
                pool.wait_ge(s_gy, n + 1)
                if k % 4 == 0:
                    pool.wait_ge(s_bx[k // 4], v * 16 + 16)
                pool.tensor_tensor(x_sb[:, k // 4, k % 4], x_sb[:, k // 4, k % 4],
                                   gate_sb[:, k // 4, k % 4], ALU.add).then_inc(s_v, 1)

            def lifted_bias(n, k):
                c = slice(k % 4, k % 4 + 1)
                pool.wait_ge(s_brstd, n + 1)
                pool.tensor_tensor(scaled_mean[:, c], mv[:, k % 4, 0:1], rstd[:, c],
                                   ALU.mult).then_inc(s_bmr, 1)
                pool.wait_ge(s_bmr, n + 1)
                pool.tensor_tensor(lift_bias[:, c], c_lift[:], scaled_mean[:, c],
                                   ALU.subtract).then_inc(s_blift, 1)

            def minus_mean(n, k):
                pool.wait_ge(s_w, n + 1)
                pool.tensor_tensor(negmu[:, k:k + 1], wsum[:, k:k + 1], c_mean[:],
                                   ALU.mult).then_inc(s_negmu, 1)

            def scale_and_bias(m, k):
                c = slice(k, k + 2)
                pool.wait_ge(s_sq, m * 2 + 2)
                pool.tensor_tensor(var2[:, c], vsum[:, c], c_epsd[:], ALU.add).then_inc(s_var2, 1)
                pool.wait_ge(s_var2, m + 1)
                pool.tensor_tensor(rnorm2[:, c], var2[:, c], c_half[:], ALU.pow).then_inc(s_rnorm2, 1)
                pool.wait_ge(s_rnorm2, m + 1)
                pool.tensor_tensor(rstd2[:, c], rnorm2[:, c], c_rootd[:], ALU.mult).then_inc(s_rstd2, 1)
                pool.wait_ge(s_rstd2, m + 1)
                pool.tensor_tensor(nbias2[:, c], negmu[:, c], rstd2[:, c], ALU.mult).then_inc(s_nb2, 1)

            def slot(n, k, v):
                if exists(n + 3):
                    rstd_of(n + 3, (k + 3) % 8, s_baggr, s_bveps, s_brstd, c_eps4)
                    lifted_bias(n + 3, (k + 3) % 8)
                if exists(n - 2):
                    minus_mean(n - 2, (k - 2) % 8)
                if exists(n + 5):
                    residual(n + 5, (k + 5) % 8, v if k < 3 else v + 1)
                if k % 2 == 0 and exists(n - 4):
                    scale_and_bias(v * 4 + k // 2 - 2, (k - 4) % 8)
            run_slots(pool, -5, TILES + 2, slot)

        @block.vector
        def _(dve):
            steps = [0]

            def wait_own(instruction):
                steps[0] += 1
                instruction.then_inc(s_dve, 1)
                dve.wait_ge(s_dve, steps[0])

            nc.vector.memset(ones_sb[:], 1.0).then_inc(s_ones, 1)
            nc.vector.memset(hd_first[:], 0.0)

            def largest(m, src):
                return nc.vector.tensor_reduce(amax[:, m:m + 1], src, AX.X, ALU.max,
                                               apply_absolute_value=True)

            def scales(a, b):
                wait_own(nc.vector.tensor_scalar(amax_pos[:, a:b], amax_all[:, a:b], 1e-30, None, ALU.max))
                wait_own(nc.vector.tensor_scalar(pow2[:, a:b].bitcast(I32), amax_pos[:, a:b].bitcast(I32),
                                                 0x7F800000, None, ALU.bitwise_and))
                wait_own(nc.vector.reciprocal(pow2_inv[:, a:b], pow2[:, a:b]))
                return nc.vector.tensor_scalar(scale[:, a:b], pow2_inv[:, a:b], SPLIT_TOP, None, ALU.mult)

            def unscales(a, b, rows):
                wait_own(nc.vector.tensor_scalar(unscale[:, a:b], pow2[:, a:b], 1.0 / (SPLIT_TOP * rows),
                                                 None, ALU.mult))

            def split(high, low, src, m):
                wait_own(nc.vector.tensor_scalar(high, src, scale[:, m:m + 1], None, ALU.mult))
                wait_own(nc.vector.scalar_tensor_tensor(low, src, scale[:, m:m + 1], high, ALU.mult,
                                                        ALU.subtract))

            def prepare_gate_weights():
                dve.wait_ge(s_small, 16)
                for i in range(2):
                    dve.wait_ge(s_wg[i], 16)
                    t = slice(i * KT // 2, (i + 1) * KT // 2)
                    last = nc.vector.tensor_reduce(row_max[:, t], wg_raw[:, t], AX.X, ALU.max,
                                                   apply_absolute_value=True)
                    if i == 0:
                        nc.vector.tensor_tensor(
                            wp_fold[:], wp_raw, gamma_sb.rearrange("p (t o) -> p t o", o=1)
                            .to_broadcast([P, KT, 2 * STATE]), ALU.mult)
                wait_own(last)
                wait_own(nc.vector.tensor_tensor(row_max_g[:], row_max[:], gamma_sb, ALU.mult))
                largest(1, wp_fold[:].rearrange("p t n -> p (t n)"))
                largest(0, row_max_g[:]).then_inc(s_amax, 1)
                a_normalise(1, 1)
                low_half(0, 0, s_hi, s_lo)
                dve.wait_ge(s_amax_all, 1)
                wait_own(scales(0, 2))
                nc.vector.tensor_scalar(g_scale[:], gamma_sb, scale[:, 0:1], None, ALU.mult).then_inc(s_scale, 1)
                wp_hi, wp_lo = wp_halves[:, :, 0], wp_halves[:, :, 1]
                wait_own(nc.vector.tensor_scalar(wp_hi, wp_fold[:], scale[:, 1:2], None, ALU.mult))
                nc.vector.scalar_tensor_tensor(wp_lo, wp_fold[:], scale[:, 1:2], wp_hi, ALU.mult,
                                               ALU.subtract)
                for t in range(KT):
                    dve.wait_ge(s_wg_hi, t + 1)
                    nc.vector.scalar_tensor_tensor(wg_lo[:, t], wg_raw[:, t], g_scale[:, t:t + 1],
                                                   wg_hi[:, t], ALU.mult, ALU.subtract).then_inc(s_wready, 1)
                for a in range(2):
                    last = nc.vector.tensor_copy(
                        wp_rep[:, a], wp_raw[:, :, a * STATE:(a + 1) * STATE]
                        .rearrange("p t (o s) -> p t o s", o=1).to_broadcast([P, KT, BATCH, STATE]))
                last.then_inc(s_wprep, 1)

            def prepare_gate_bias():
                unscales(0, 2, ROW_SCALE)
                dve.wait_ge(s_bias_mm, 1)
                wait_own(nc.vector.tensor_copy(gbias_sb[:], bank[7][:]))

            def prepare_biases():
                dve.wait_ge(s_bias_mm, 2)
                wait_own(nc.vector.tensor_scalar(fbias_sb[:], bank[6][:], 1.0 / (LIFT * D),
                                                 None, ALU.mult))
                wait_own(nc.vector.tensor_tensor(zbias[:], bank[5][:, 0:2], small_sb[:, W_BIAS:W_BIAS + 2],
                                                 ALU.add))
                nc.vector.sem_inc(s_zbias, 1)
                dve.wait_ge(s_cst, 16)
                dve.wait_ge(s_a_c, 16)
                nc.vector.tensor_tensor(scan_a[:], a_rep, cst[:, C_BLOCKS:C_BLOCKS + P], ALU.mult)
                largest(2, c_rep).then_inc(s_amax, 1)

            def split_c():
                dve.wait_ge(s_amax_all, 2)
                wait_own(scales(2, 3))
                unscales(2, 3, 2 * STATE_SCALE)
                wait_own(nc.vector.tensor_scalar(c_hi[:], c_rep, scale[:, 2:3], None, ALU.mult))
                wait_own(nc.vector.scalar_tensor_tensor(c_lo[:], c_rep, scale[:, 2:3], c_hi[:], ALU.mult,
                                                        ALU.subtract))
                nc.vector.sem_inc(s_c_split, 1)

            def c_parts_of(j, low):
                column = C_PARTS + 2 * j + low
                mask = cst[:, column:column + 1]
                if not low:
                    wait_own(nc.vector.tensor_scalar(c_parts[:, j], c_hi[:], mask, None, ALU.mult))
                else:
                    nc.vector.scalar_tensor_tensor(c_parts[:, j], c_lo[:], mask, c_parts[:, j], ALU.mult,
                                                   ALU.add)

            def largest_bias():
                wait_own(nc.vector.tensor_reduce(bias_max[:], fbias_sb[:], AX.X, ALU.max,
                                                 apply_absolute_value=True))

            def transform_bias(t):
                if t == 0:
                    dve.wait_ge(s_wb, 16 * len(WB_LOADS))
                    dve.wait_ge(s_folded, 2)
                nc.vector.scalar_tensor_tensor(
                    fbias_sb[:, 0:HALF], cos_sb[:, t], 1.0, fbias_even[:], ALU.mult, ALU.mult,
                    accum_out=shift[:, 0, t:t + 1])
                wait_own(nc.vector.scalar_tensor_tensor(
                    fbias_sb[:, HALF:D], sin_sb[:, t, 1:HALF - 1], 1.0, fbias_odd[:, 1:HALF - 1],
                    ALU.mult, ALU.mult, accum_out=shift[:, 1, t:t + 1]))

            def sum_weights():
                dve.wait_ge(s_w_abs, 4)
                nc.vector.tensor_reduce(w_max[:], w_abs[:], AX.X, ALU.max)
                nc.vector.tensor_reduce(w_abs_sum[:], w_abs[:], AX.X, ALU.add).then_inc(s_w_abs_sum, 1)

            def scale_of_w():
                dve.wait_ge(s_w_abs_all, 2)
                wait_own(nc.vector.tensor_scalar(w_max[:], w_max_all[:], 1e-30, None, ALU.max))
                wait_own(nc.vector.tensor_scalar(w_pow2[:].bitcast(I32), w_max[:].bitcast(I32), 0x7F800000,
                                                 None, ALU.bitwise_and))
                wait_own(nc.vector.reciprocal(w_max[:], w_pow2[:]))
                nc.vector.tensor_scalar(w_scale[:], w_max[:], SPLIT_TOP, None, ALU.mult).then_inc(s_w_scale, 1)

            def bias_shift():
                flat = shift[:].rearrange("p a t -> p (a t)")
                nc.vector.tensor_tensor(flat, flat, small_sb[:, W_ROW0:W_ROW0 + 2 * KT], ALU.subtract)

            def scale_of_m():
                wait_own(nc.vector.scalar_tensor_tensor(amax_all[:, 3:4], w_abs_all[:], 2.0 / D, bias_max[:],
                                                        ALU.mult, ALU.add))
                wait_own(scales(3, 4))

            def scale_of_p():
                wait_own(nc.vector.tensor_scalar(p_scale[:], scale[:, 3:4], 1.0 / D, None, ALU.mult))
                wait_own(nc.vector.scalar_tensor_tensor(
                    p_ratio[:, 0:1], w_pow2[:], 1.0 / (SPLIT_TOP * WAVE_SCALE), p_scale[:], ALU.mult,
                    ALU.mult))
                nc.vector.tensor_scalar(p_ratio[:, 1:2], p_ratio[:, 0:1], -1.0, None, ALU.mult)
                flat = shift[:].rearrange("p a t -> p (a t)")
                wait_own(nc.vector.tensor_scalar(flat, flat, p_scale[:], None, ALU.mult))
                nc.vector.sem_inc(s_mscale, 1)
                unscales(3, 4, ROW_SCALE)

            def frequency_weights_low(i):
                dve.wait_ge(s_w_hi, i + 1)
                w, halves = ((w_re_sb, w_re_halves), (w_im_sb, w_im_halves))[i // KT]
                nc.vector.scalar_tensor_tensor(halves[1][:, i % KT], w[:, i % KT], w_scale[:, 0:1],
                                               halves[0][:, i % KT], ALU.mult,
                                               ALU.subtract).then_inc(s_w_lo, 1)

            def aggregate(n, k, aggr_done):
                nc.vector.bn_aggr(mv[:, k % 4], bn[:, k % 4]).then_inc(aggr_done, 1)

            def a_statistics(n, k, v):
                if isinstance(n, int) and n == 0:
                    dve.wait_ge(s_xfirst, 16)
                elif k % 4 == 0 or isinstance(n, int) and n == 2:
                    dve.wait_ge(s_xl[k // 4], v * 16 + 16)
                nc.vector.bn_stats(bn[:, k % 4], x_sb[:, k // 4, k % 4]).then_inc(s_bn, 1)

            def a_normalise(n, k):
                dve.wait_ge(s_rstd, n + 1)
                if before(n, 4):
                    dve.wait_ge(s_t, n - 3)
                nc.vector.tensor_scalar(norm_sb[:, k % 4], x_sb[:, k // 4, k % 4], mv[:, k % 4, 0:1],
                                        rstd[:, k % 4:k % 4 + 1], ALU.subtract,
                                        ALU.mult).then_inc(s_norm, 1)

            def low_half(n, k, hi_done, lo_done):
                dve.wait_ge(hi_done, n + 1)
                nc.vector.scalar_tensor_tensor(lo_sb[:, k % 2].rearrange("p t r -> p (t r)"), ps_t[k % 2][:],
                                               ROW_SCALE, hi_sb[:, k % 2].rearrange("p t r -> p (t r)"),
                                               ALU.mult, ALU.subtract).then_inc(lo_done, 1)

            def gate_logits(n, k):
                dve.wait_ge(s_gate, n + 1)
                if before(n, 2):
                    dve.wait_ge(s_gsig, n - 1)
                nc.vector.scalar_tensor_tensor(gsum_sb[:, k % 2], ps_g[k % 2][:], unscale[:, 0:1],
                                               gbias_sb[:], ALU.mult, ALU.add).then_inc(s_gsum, 1)

            def sum_zrow(v, q):
                dve.wait_ge(s_zlow, v * 2 + q + 1)
                if q == 0 and before(v, 1):
                    dve.wait_ge(s_zt, v)
                nc.vector.tensor_tensor(
                    zrow[:, :, 4 * q:4 * q + 4].rearrange("p a b s -> p b a s"),
                    z_parts(q)[:, :, 0].rearrange("p b (a s) -> p b a s", a=2),
                    z_low[:, q].rearrange("p b (a s) -> p b a s", a=2), ALU.add).then_inc(s_zrow, 1)

            def copy_z(v):
                dve.wait_ge(s_del, v + 1)
                nc.vector.tensor_scalar(z_sb[:, bass.ts(v, P)], ps_x[:, P:2 * P], unscale[:, 1:2],
                                        zbias[:, 1:2], ALU.mult, ALU.add).then_inc(s_z, 1)

            def slot(n, k, v):
                if isinstance(n, int) and n == -1:
                    prepare_gate_weights()
                if isinstance(n, int) and n == 1:
                    prepare_gate_bias()
                if k == 4 and exists(n - 8):
                    copy_z(v - 1)
                if exists(n + 3):
                    a_statistics(n + 3, (k + 3) % 8, v if k < 5 else v + 1)
                if exists(n + 3):
                    dve.wait_ge(s_bn, n + 4)
                if exists(n + 2) and not (isinstance(n, int) and n == -1):
                    a_normalise(n + 2, (k + 2) % 8)
                if exists(n + 3):
                    aggregate(n + 3, (k + 3) % 8, s_aggr)
                if exists(n + 1) and not (isinstance(n, int) and n == -1):
                    low_half(n + 1, k + 1, s_hi, s_lo)
                if exists(n - 1):
                    gate_logits(n - 1, (k - 1) % 8)
                if k % 4 == 1 and exists(n - 4):
                    sum_zrow(v if k == 5 else v - 1, 0 if k == 5 else 1)
                if isinstance(n, int) and n in (1, 3, 4):
                    {1: prepare_biases, 3: split_c, 4: largest_bias}[n]()
                if isinstance(n, int) and 5 <= n < 8:
                    transform_bias(n - 5)
                if isinstance(n, int) and n == TILES - 8:
                    sum_weights()
                if isinstance(n, int) and n == TILES - 7:
                    scale_of_w()
                if isinstance(n, int) and TILES - 6 <= n < TILES:
                    m = n - TILES + 6
                    for i in range(m, m + 1) if m < 4 else range(2 * m - 4, 2 * m - 2):
                        frequency_weights_low(i)
                if isinstance(n, int) and n == TILES + 3:
                    scale_of_m()
                if isinstance(n, int) and n == TILES - 4:
                    transform_bias(3)
                    bias_shift()
            run_slots(dve, -3, TILES + 4, slot)

            def combine(q):
                dve.wait_ge(s_mm, products_with(2 * q + 1))
                dve.wait_ge(s_even, q + 1)
                even, odd, i = even_sb[:, q % 2], bank[3 + 2 * (q % 2)], q // 2
                sign = 1 if q < 2 * KT and q % 2 == 0 else -1
                if q < 2 * KT:
                    if q >= 2:
                        dve.wait_ge(s_pair, q - 1)
                    dst, done = pq_sb[:, q % 2], s_pfull
                    ratio = {1: p_ratio[:, 0:1], -1: p_ratio[:, 1:2]}
                else:
                    dst, done = m_sb[:, q - 2 * KT], s_pair
                    ratio = {1: 1.0 / WAVE_SCALE, -1: -1.0 / WAVE_SCALE}
                nc.vector.scalar_tensor_tensor(dst[:, 0:HALF], odd[:, 0:HALF], ratio[sign], even, ALU.mult,
                                               ALU.add)
                nc.vector.scalar_tensor_tensor(dst[:, HALF:D], odd[:, HALF - 2:0:-1], ratio[-sign],
                                               even[:, HALF - 2:0:-1], ALU.mult, ALU.add).then_inc(done, 1)

            def beside_step(k):
                if k in combined_beside:
                    combine(combined_beside[k])
                if k in (2, 4, 6, 8):
                    c_parts_of((k - 2) // 4, (k // 2 + 1) % 2)

            def compare(r):
                nc.vector.tensor_tensor(differ[:], last_step, ends[:], ALU.not_equal).then_inc(s_dscan, 1)
                dve.wait_ge(s_dscan, r)
                nc.vector.tensor_reduce(n_differ[:], differ[:], AX.X, ALU.add).then_inc(s_cmp, 1)
                dve.wait_ge(s_cnt, r)
                nc.vector.tensor_copy(flag[:], bank[0][0:1, 0:1]).then_inc(s_flag, 1)
                dve.wait_ge(s_flag, r)
                nc.vector.sem_inc(s_round_dve, 1)

            last_step = h_sb[:, CHUNK - 1::CHUNK]

            def scan_round(k0, first=False):
                if not first:
                    dve.wait_ge(s_h, k0)
                    nc.vector.tensor_tensor(hd_first[:, 1:LANES], h_sb[:, CHUNK - 1:SEQ - CHUNK:CHUNK],
                                            del_sb[:, CHUNK::CHUNK], ALU.mult).then_inc(s_hd, 1)
                    nc.vector.tensor_copy(ends[:], last_step)
                for s in range(CHUNK):
                    dve.wait_ge(s_h, k0 + s + 1)
                    if s + 1 < CHUNK:
                        nc.vector.tensor_tensor(hd[:], h_sb[:, s::CHUNK], del_sb[:, s + 1::CHUNK],
                                                ALU.mult).then_inc(s_hd, 1)
                    if isinstance(k0, int):
                        beside_step(k0 + s)
                    if not first:
                        dve.wait_ge(s_high, k0 - CHUNK + s + 1)
                        last = nc.vector.scalar_tensor_tensor(h_lo[:, s::CHUNK], h_sb[:, s::CHUNK],
                                                              STATE_SCALE, h_hi[:, s::CHUNK], ALU.mult,
                                                              ALU.subtract)
                if not first:
                    last.then_inc(s_split, 1)

            dve.wait_ge(s_del, OCTETS)
            nc.vector.sem_inc(s_hd, 1)
            scale_of_p()
            scan_round(0, first=True)
            scan_round(CHUNK)
            compare(1)
            changed = dve.value_load(flag[0:1, 0:1])
            if STEPS in combined_beside:
                combine(combined_beside[STEPS])
            with dve.If(changed > 0):
                for r in range(BATCH // 2):
                    dve.wait_ge(s_hrep[r], 4 * 16)
                dve.wait_ge(s_seen, 1)
                with dve.Fori(2, LANES) as r:
                    again = dve.value_load(flag[0:1, 0:1])
                    with dve.If(again > 0):
                        scan_round(r * CHUNK)
                        dve.wait_ge(s_split, r)
                        compare(r)
                nc.vector.sem_inc(s_final, 1)

            def low_m(i):
                dve.wait_ge(s_m_hi, i + 1)
                nc.vector.tensor_tensor(m_lo[:, i], m_sb[:, i], m_hi[:, i],
                                        ALU.subtract).then_inc(s_msplit, 1)

            def gated(n, k, v):
                dve.wait_ge(s_y, n + 1)
                if k % 4 == 0:
                    dve.wait_ge(s_bg[k // 4], v * 16 + 16)
                nc.vector.scalar_tensor_tensor(gate_sb[:, k // 4, k % 4], ps_y[k % 2][:], unscale[:, 2:3],
                                               gate_sb[:, k // 4, k % 4], ALU.mult,
                                               ALU.mult).then_inc(s_gy, 1)

            def b_statistics(n, k):
                dve.wait_ge(s_v, n + 1)
                nc.vector.bn_stats(bn[:, k % 4], x_sb[:, k // 4, k % 4]).then_inc(s_bbn, 1)

            def ffn_sum(n, k):
                dve.wait_ge(s_f, n + 1)
                if before(n, 8):
                    dve.wait_ge(s_out, n - 7)
                nc.vector.scalar_tensor_tensor(w_ring[:, k], ps_g[k % 2][:], unscale[:, 3:4],
                                               norm_sb[:, k % 4], ALU.mult, ALU.add,
                                               accum_out=wsum[:, k:k + 1]).then_inc(s_w, 1)

            def slot(n, k, v):
                if exists(n + 4):
                    b_statistics(n + 4, (k + 4) % 8)
                    dve.wait_ge(s_bbn, n + 5)
                if exists(n + 1):
                    low_half(n + 1, k + 1, s_bhi, s_blo)
                if exists(n + 4):
                    aggregate(n + 4, (k + 4) % 8, s_baggr)
                if exists(n + 6):
                    gated(n + 6, (k + 6) % 8, v if k < 2 else v + 1)
                if exists(n - 1):
                    ffn_sum(n - 1, (k - 1) % 8)
                if isinstance(n, int) and n in (-5, -3):
                    combine(2 * KT + 2 if n == -5 else 2 * KT + 3)
                if isinstance(n, int) and n in (-6, -4, -2, -1):
                    low_m((-6, -4, -2, -1).index(n))
            run_slots(dve, -6, TILES, slot)
            dve.wait_ge(s_nb2, TILES // 2)
            nc.vector.tensor_scalar(out_sb[:, 1, 3], w_ring[:, 7], rstd2[:, 7:8], nbias2[:, 7:8], ALU.mult,
                                    ALU.add).then_inc(s_out_last, 1)

        @block.tensor
        def _(pe):
            def gate_bias_products():
                pe.wait_ge(s_brep, 1)
                pe.wait_ge(s_brow, 16)
                for t in range(KT):
                    if t % (KT // 2) == 0:
                        pe.wait_ge(s_wg[t // (KT // 2)], 16)
                    nc.tensor.matmul(bank[7][:], beta_rep[:, t], wg_raw[:, t], start=(t == 0), stop=False)
                nc.tensor.matmul(bank[7][:], ones_sb[0:1, :], bias_row[0:1, 0, :], start=False,
                                 stop=True).then_inc(s_bias_mm, 1)

            def other_bias_products():
                pe.wait_ge(s_wprep, 1)
                nc.tensor.matmul(bank[6][:], ones_sb[0:1, :], bias_row[0:1, 1, :], start=True, stop=True)
                for a in range(2):
                    for t in range(KT):
                        last = nc.tensor.matmul(bank[5][:, a:a + 1],
                                                wp_rep[:, a, t].rearrange("p b s -> p (b s)"),
                                                beta_sb[:, t:t + 1], start=(t == 0), stop=(t == KT - 1))
                last.then_inc(s_bias_mm, 1)

            def transpose(n, k, norm_done, hi_done, lo_done, t_done):
                pe.wait_ge(norm_done, n + 1)
                if before(n, 2):
                    pe.wait_ge(hi_done, n - 1)
                    pe.wait_ge(lo_done, n - 1)
                for t in range(KT):
                    last = nc.tensor.transpose(ps_t[k % 2][:, t * P:(t + 1) * P],
                                               norm_sb[:, k % 4, t * P:(t + 1) * P], ident)
                last.then_inc(t_done, 1)

            def product(dst, k, w_hi, w_lo, split=None):
                for t in range(KT):
                    if split is not None:
                        pe.wait_ge(split, t + 1)
                    nc.tensor.matmul(dst, hi_sb[:, k % 2, t], w_hi[:, t], start=(t == 0), stop=False)
                    nc.tensor.matmul(dst, hi_sb[:, k % 2, t], w_lo[:, t], start=False, stop=False)
                for t in range(KT):
                    last = nc.tensor.matmul(dst, lo_sb[:, k % 2, t], w_hi[:, t], start=False,
                                            stop=(t == KT - 1))
                return last

            pe.wait_ge(s_cst, 16)

            def products(n, k, v):
                pe.wait_ge(s_hi, n + 1)
                pe.wait_ge(s_lo, n + 1)
                if before(n, 2):
                    pe.wait_ge(s_gsum, n - 1)
                first = isinstance(n, int) and n == 0
                product(ps_g[k % 2][:], k, wg_hi, wg_lo, s_wready if first else None).then_inc(s_gate, 1)
                q, b = k // 4, k % 4
                if b == 0 and before(n, 8):
                    pe.wait_ge(s_zrow, v * 2 + q - 1)
                if isinstance(n, int) and n == 4:
                    pe.wait_ge(s_zbias, 1)
                z = z_parts(q)[:, b].rearrange("p h n -> p (h n)")
                for t in range(KT):
                    nc.tensor.matmul(z, hi_sb[:, k % 2, t], wp_halves[:, t].rearrange("p h n -> p (h n)"),
                                     start=(t == 0), stop=False)
                for t in range(KT):
                    last = nc.tensor.matmul(z[:, 0:2 * STATE], lo_sb[:, k % 2, t], wp_halves[:, t, 0],
                                            start=False, stop=(t == KT - 1))
                last.then_inc(s_proj, 1)

            def fourier_matmul(m):
                j, t, half = ORDER[m // PRODUCT], m % PRODUCT // 3, m % 3
                q = j // 2
                if q < 2 * KT:
                    i = q // 2
                    w = ((w_re_halves, w_im_halves), (w_im_halves, w_re_halves))[q % 2][j % 2]
                else:
                    i = q - 2 * KT
                    w = (pt_halves, qt_halves)[j % 2]
                    if m % PRODUCT == 0 and i == 0:
                        pe.wait_ge(s_pair, 2 * KT - 1 + j % 2)
                if m % PRODUCT == 0 and q >= 2:
                    pe.wait_ge(s_pfull if q - 2 < 2 * KT else s_pair, q - 1)
                w_half, f_half = ((0, 0), (0, 1), (1, 0))[half]
                last = nc.tensor.matmul(bank[2 + 2 * (q % 2) + j % 2][:, 0:HALF],
                                        w[w_half][:, t, i * P:(i + 1) * P],
                                        (cos_halves, sin_halves)[j % 2][:, t, f_half],
                                        start=(m % PRODUCT == 0), stop=(m % PRODUCT == PRODUCT - 1))
                if m % PRODUCT == PRODUCT - 1:
                    last.then_inc(s_mm, 1)

            def fourier_product(j):
                for m in range(PRODUCT * j, PRODUCT * (j + 1)):
                    fourier_matmul(m)

            def z_transpose(v):
                pe.wait_ge(s_zrow, v * 2 + 2)
                if before(v, 1):
                    pe.wait_ge(s_z, v)
                for a in range(2):
                    last = nc.tensor.transpose(ps_x[:, a * P:(a + 1) * P],
                                               zrow[:, a].rearrange("p b s -> p (b s)"), ident)
                last.then_inc(s_zt, 1)

            def slot(n, k, v):
                if exists(n + 1):
                    transpose(n + 1, k + 1, s_norm, s_hi, s_lo, s_t)
                if isinstance(n, int) and n == -1:
                    gate_bias_products()
                if k == 2 and exists(n - 8):
                    z_transpose(v - 1)
                if exists(n):
                    products(n, k, v)
                if isinstance(n, int) and n == 0:
                    other_bias_products()
                if isinstance(n, int) and n == TILES:
                    pe.wait_ge(s_wb, 16 * len(WB_LOADS))
                    pe.wait_ge(s_w_lo, 2 * KT)
                    pe.wait_ge(s_gsum, TILES - 1)
                    fourier_product(0)
                if isinstance(n, int) and n == TILES + 2:
                    pe.wait_ge(s_gsum, TILES)
                    fourier_product(1)
            run_slots(pe, -1, TILES + 2, slot)

            pe.wait_ge(s_lo, TILES)
            pe.wait_ge(s_z, OCTETS)

            def scan_round(k0, first=False):
                def inputs(s):
                    nc.tensor.matmul(bank[s % 2][:, 0:LANES], ident, z_sb[:, s::CHUNK],
                                     start=True, stop=False)
                if not first:
                    pe.wait_ge(s_h, k0)
                inputs(0)
                for s in range(CHUNK):
                    pe.wait_ge(s_hd, k0 + s + 1)
                    nc.tensor.matmul(bank[s % 2][:, 0:LANES], scan_a[:], (hd if s else hd_first)[:],
                                     start=False, stop=True).then_inc(s_pre, 1)
                    if s + 1 < CHUNK:
                        inputs(s + 1)
                    if isinstance(k0, int):
                        step = k0 + s
                        for m in range(matmuls_until[step - 1] if step else 2 * PRODUCT, matmuls_until[step]):
                            fourier_matmul(m)

            def count_changes(r):
                pe.wait_ge(s_cmp, r)
                nc.tensor.matmul(bank[0][0:1, 0:1], n_differ[:], ones_sb[:, 0:1], start=True,
                                 stop=True).then_inc(s_cnt, 1)
                if isinstance(r, int):
                    fourier_product(LATE)
                pe.wait_ge(s_flag, r)

            scan_round(0, first=True)
            scan_round(CHUNK)
            count_changes(1)
            changed = pe.value_load(flag[0:1, 0:1])
            with pe.If(changed > 0):
                with pe.Fori(2, LANES) as r:
                    again = pe.value_load(flag[0:1, 0:1])
                    with pe.If(again > 0):
                        scan_round(r * CHUNK)
                        count_changes(r)
                for r in range(BATCH // 2):
                    pe.wait_ge(s_hrep2[r], 4 * 16)

            pe.wait_ge(s_split, 1)
            pe.wait_ge(s_c_first, 2 * BATCH)

            def first_states_out(n, k):
                if before(n, 2):
                    pe.wait_ge(s_gy, n - 1)
                halves = ((h_hi, 0), (h_hi, 1), (h_lo, 0))
                for i, (h, c) in enumerate(halves):
                    last = nc.tensor.matmul(ps_y[k % 2][:], h[:, 0:P], c_first[:, n, c],
                                            start=(i == 0), stop=(i == len(halves) - 1))
                last.then_inc(s_y, 1)

            def states_out(n, k, v):
                if isinstance(n, int) and n < 16 and n % 2 == 0:
                    pe.wait_ge(s_hrep[k // 2], 4 * 16)
                if before(n, 2):
                    pe.wait_ge(s_gy, n - 1)
                nc.tensor.matmul(ps_y[k % 2][:], h_rep[:, k // 2, bass.ts(v, P)], c_parts[:, k % 2],
                                 start=True, stop=True).then_inc(s_y, 1)

            def ffn(n, k):
                pe.wait_ge(s_bhi, n + 1)
                pe.wait_ge(s_blo, n + 1)
                if before(n, 2):
                    pe.wait_ge(s_w, n - 1)
                first = isinstance(n, int) and n == 0
                product(ps_g[k % 2][:], k, m_hi, m_lo, s_msplit if first else None).then_inc(s_f, 1)

            def slot(n, k, v):
                if exists(n + 1):
                    transpose(n + 1, k + 1, s_bnorm, s_bhi, s_blo, s_bt)
                if isinstance(n, int) and n + 7 < 8:
                    first_states_out(n + 7, (k + 7) % 8)
                elif exists(n + 7):
                    states_out(n + 7, (k + 7) % 8, v if k < 1 else v + 1)
                if isinstance(n, int) and n < 0 and LATE + n + 7 in range(LATE + 1, 2 * PAIRS):
                    fourier_product(LATE + n + 7)
                if exists(n):
                    ffn(n, k)
            run_slots(pe, -7, TILES - 1, slot)


def shape_constants():
    c = np.zeros((P, C_WIDTH), np.float32)
    c[:, C_IDENT:C_IDENT + P] = np.eye(P)
    c[:, C_BLOCKS:C_BLOCKS + P] = np.kron(np.eye(BATCH), np.ones((STATE, STATE)))
    row = np.arange(P)
    for j in range(2):
        for low in range(2):
            c[:, C_PARTS + 2 * j + low] = (row // STATE % 2 == j) & (row // 32 % 2 == low)
    return c


def packed_weights(gamma, beta, b_delta, b_in, w_delta, w_in, w_real, w_imag):
    def columns(w):
        return w.reshape(KT, P, -1).transpose(1, 0, 2).reshape(P, -1)

    biases = np.stack([np.tile(b_delta, BATCH), np.tile(b_in, BATCH)], axis=1)
    projections = columns(np.concatenate([w_delta, w_in], axis=1))
    return np.ascontiguousarray(np.concatenate(
        [columns(gamma), columns(beta), biases, projections, columns(w_real[0]), columns(w_imag[0])],
        axis=1))


def fourier_constants():
    jk = np.outer(np.arange(D), np.arange(HALF)) % D
    a = 2.0 * np.pi * jk / D
    return np.stack([np.cos(a), np.sin(a)])


def fourier_halves():
    c = fourier_constants() * WAVE_SCALE
    high = c.astype(np.float16)
    return np.stack([high, (c - high).astype(np.float16)], axis=2)


def kernel(**inputs):
    import concourse.bacc as _bacc
    from concourse.bass_utils import run_bass_kernel_spmd as _run

    nc = _bacc.Bacc("TRN2", target_bir_lowering=False, num_devices=1)
    a = {name.removeprefix("L0_"): np.asarray(value) for name, value in inputs.items()}
    arrays = {
        "x": np.ascontiguousarray(a["attn_x"]).reshape(BATCH * SEQ, D),
        "small_weights": packed_weights(*(a["attn_" + name] for name in (
            "ln_gamma", "ln_beta", "b_delta", "b_in", "w_delta", "w_in")),
            a["ffn_w_freq_real"], a["ffn_w_freq_imag"]),
        "a_and_c": np.concatenate([np.tile(a["attn_A"], (BATCH, BATCH)), np.tile(a["attn_C"], (BATCH, 1))],
                                  axis=1),
        "bias_rows": np.stack([a["attn_b_gate"], a["ffn_bias"]])[None],
        "w_gate": np.ascontiguousarray(a["attn_w_gate"]),
        "w_freq_real": np.ascontiguousarray(a["ffn_w_freq_real"]),
        "w_freq_imag": np.ascontiguousarray(a["ffn_w_freq_imag"]),
        "shape_constants": shape_constants(),
        "fourier_constants": fourier_constants().astype(np.float32),
        "fourier_halves": fourier_halves(),
    }
    args = [nc.dram_tensor(k, a.shape, mybir.dt.from_np(a.dtype), kind="ExternalInput").ap()
            for k, a in arrays.items()]
    out = nc.dram_tensor("out", (BATCH * SEQ, D), F32, kind="ExternalOutput").ap()
    gate_dram = nc.dram_tensor("gate_dram", (BATCH * SEQ, D), F32, kind="Internal").ap()
    build(nc, *args, out, gate_dram)
    r = _run(nc, [arrays], core_ids=[0])
    return r.results[0]["out"].reshape(BATCH, SEQ, D)
```
